# Optimizing a Trainium2 kernel written in Bass

```python
import numpy as np
import jax
import jax.numpy as jnp

def _softmax(x, axis=-1):
    return jax.nn.softmax(x, axis=axis)

def _gelu(x):
    return jax.nn.gelu(x, approximate=True)

def _silu(x):
    return jax.nn.silu(x)

def _sigmoid(x):
    return jax.nn.sigmoid(x)

def _layernorm(x, axis=-1, eps=1e-05):
    m = jnp.mean(x, axis=axis, keepdims=True)
    v = jnp.var(x, axis=axis, keepdims=True)
    return (x - m) / jnp.sqrt(v + eps)

def _scatter_add(tgt, idx, src, axis=0):
    return tgt.at[idx].add(src)

def _segment_sum(src, seg, n):
    return jax.ops.segment_sum(src, seg, n)
kernel_name = 'mk_seq_postln_d1_jaxref_r4_eec7fc'

def setup_inputs(seed: int=0):
    np.random.seed(seed)
    _w = jnp.asarray

    def _L0_attn_setup():
        import jax, jax.numpy as jnp
        import numpy as np
        B, T, C = (2, 512, 256)
        N_HEAD = 16
        HEAD_DIM = C // N_HEAD
        ATTN_MODE = 'local'
        LOCAL_ATTN_CTX = 64

        def build_mask(n, attn_mode, local_attn_ctx):
            i = jnp.arange(n)[:, None]
            j = jnp.arange(n)[None, :]
            causal = j <= i
            if attn_mode == 'all':
                return causal
            if attn_mode == 'local':
                return causal & (j >= i - local_attn_ctx)
            if attn_mode == 'strided':
                return causal & (j % local_attn_ctx == 0)
            raise ValueError(attn_mode)
        key = jax.random.key(seed)
        k1, k2, k3 = jax.random.split(key, 3)
        s = 0.02
        return {'x': jax.random.normal(k1, (B, T, C), dtype=jnp.float32), 'W_attn': jax.random.normal(k2, (C, 3 * C), dtype=jnp.float32) * s, 'b_attn': jnp.zeros((3 * C,), dtype=jnp.float32), 'W_proj': jax.random.normal(k3, (C, C), dtype=jnp.float32) * s, 'b_proj': jnp.zeros((C,), dtype=jnp.float32)}
    _L0_attn_in = _L0_attn_setup()

    def _L0_ffn_setup():
        import jax, jax.numpy as jnp
        import numpy as np
        LN_EPS = 1e-12
        key = jax.random.key(seed)
        ks = jax.random.split(key, 8)
        B, S, H, I, E = (4, 512, 256, 1024, 8)
        sH = 1.0 / np.sqrt(H)
        sI = 1.0 / np.sqrt(I)
        return {'hidden_states': jax.random.normal(ks[0], (B, S, H), dtype=jnp.float32), 'Wr': jax.random.uniform(ks[1], (E, H), jnp.float32, -sH, sH), 'W1': jax.random.uniform(ks[2], (E, H, I), jnp.float32, -sH, sH), 'b1': jax.random.uniform(ks[3], (E, I), jnp.float32, -sH, sH), 'Wo': jax.random.uniform(ks[4], (I, H), jnp.float32, -sI, sI), 'bo': jax.random.uniform(ks[5], (H,), jnp.float32, -sI, sI), 'gamma': jnp.ones((H,), jnp.float32), 'beta': jnp.zeros((H,), jnp.float32)}
    _L0_ffn_in = _L0_ffn_setup()
    _d = {'L0_attn_x': _L0_attn_in['x'], 'L0_attn_W_attn': _L0_attn_in['W_attn'], 'L0_attn_b_attn': _L0_attn_in['b_attn'], 'L0_attn_W_proj': _L0_attn_in['W_proj'], 'L0_attn_b_proj': _L0_attn_in['b_proj'], 'L0_ffn_Wr': _L0_ffn_in['Wr'], 'L0_ffn_W1': _L0_ffn_in['W1'], 'L0_ffn_b1': _L0_ffn_in['b1'], 'L0_ffn_Wo': _L0_ffn_in['Wo'], 'L0_ffn_bo': _L0_ffn_in['bo'], 'L0_ffn_gamma': _L0_ffn_in['gamma'], 'L0_ffn_beta': _L0_ffn_in['beta']}
    _x0 = _d['L0_attn_x']
    _d['L0_attn_x'] = jax.random.normal(jax.random.fold_in(jax.random.key(seed), 1), (2, 2048, 256), dtype=_x0.dtype)
    del _x0
    return _d

def reference(L0_attn_x, L0_attn_W_attn, L0_attn_b_attn, L0_attn_W_proj, L0_attn_b_proj, L0_ffn_Wr, L0_ffn_W1, L0_ffn_b1, L0_ffn_Wo, L0_ffn_bo, L0_ffn_gamma, L0_ffn_beta):

    def _L0_attn_ref(x, W_attn, b_attn, W_proj, b_proj):
        import jax, jax.numpy as jnp
        import numpy as np
        B, T, C = (2, 512, 256)
        N_HEAD = 16
        HEAD_DIM = C // N_HEAD
        ATTN_MODE = 'local'
        LOCAL_ATTN_CTX = 64

        def build_mask(n, attn_mode, local_attn_ctx):
            i = jnp.arange(n)[:, None]
            j = jnp.arange(n)[None, :]
            causal = j <= i
            if attn_mode == 'all':
                return causal
            if attn_mode == 'local':
                return causal & (j >= i - local_attn_ctx)
            if attn_mode == 'strided':
                return causal & (j % local_attn_ctx == 0)
            raise ValueError(attn_mode)
        b, t, c = x.shape
        qkv = x @ W_attn + b_attn
        q, k, v = jnp.split(qkv, 3, axis=-1)

        def heads(a):
            return a.reshape(b, t, N_HEAD, HEAD_DIM).transpose(0, 2, 1, 3)
        q, k, v = (heads(q), heads(k), heads(v))
        scale = 1.0 / np.sqrt(HEAD_DIM)
        scores = jnp.einsum('bhtd,bhsd->bhts', q, k) * scale
        mask = build_mask(t, ATTN_MODE, LOCAL_ATTN_CTX)
        scores = jnp.where(mask[None, None], scores, -jnp.inf)
        attn = jax.nn.softmax(scores, axis=-1)
        out = jnp.einsum('bhts,bhsd->bhtd', attn, v)
        out = out.transpose(0, 2, 1, 3).reshape(b, t, c)
        return out @ W_proj + b_proj

    def _L0_ffn_ref(hidden_states, Wr, W1, b1, Wo, bo, gamma, beta):
        import jax, jax.numpy as jnp
        import numpy as np
        LN_EPS = 1e-12
        B, S, H = hidden_states.shape
        E = Wr.shape[0]
        x = hidden_states.reshape(-1, H)
        router_logits = x @ Wr.T
        expert_idx = jnp.argmax(jax.nn.softmax(router_logits, axis=-1), axis=-1)
        inter = jnp.zeros((x.shape[0], W1.shape[2]), dtype=x.dtype)
        for e in range(E):
            mask = (expert_idx == e)[:, None].astype(x.dtype)
            inter = inter + mask * jax.nn.gelu(x @ W1[e] + b1[e], approximate=False)
        y = inter @ Wo + bo + x
        mu = jnp.mean(y, axis=-1, keepdims=True)
        var = jnp.mean(jnp.square(y - mu), axis=-1, keepdims=True)
        out = (y - mu) * jax.lax.rsqrt(var + LN_EPS) * gamma + beta
        return out.reshape(B, S, H)
    x = L0_attn_x
    x = _layernorm(x + _L0_attn_ref(x, L0_attn_W_attn, L0_attn_b_attn, L0_attn_W_proj, L0_attn_b_proj), axis=-1)
    x = _layernorm(x + _L0_ffn_ref(x, L0_ffn_Wr, L0_ffn_W1, L0_ffn_b1, L0_ffn_Wo, L0_ffn_bo, L0_ffn_gamma, L0_ffn_beta), axis=-1)
    return x

_drawn_inputs = setup_inputs


def setup_inputs(seed=0):
    import zlib

    import numpy as np

    out = dict(_drawn_inputs(seed))
    spreads = {'L0_attn_b_attn': (0.0, 0.1),
     'L0_attn_b_proj': (0.0, 0.1),
     'L0_ffn_gamma': (1.0, 0.2),
     'L0_ffn_beta': (0.0, 0.1)}
    factors = {'L0_attn_W_attn': 3.177, 'L0_ffn_b1': 8.0, 'L0_ffn_bo': 5.907}
    for name, (base, spread) in spreads.items():
        noise = np.random.default_rng([zlib.crc32(name.encode()), seed]).standard_normal(out[name].shape)
        drawn = base * np.exp(spread * noise) if base else spread * noise
        out[name] = jnp.asarray(drawn.astype(out[name].dtype))
    for name, factor in factors.items():
        out[name] = (out[name] * factor).astype(out[name].dtype)
    return out
```

```python
import concourse.bass as bass
from concourse import mybir
from contextlib import ExitStack


def attention_then_routed_ffn(
    nc: bass.Bass,
    x: bass.AP,
    w_attn: bass.AP,
    b_attn: bass.AP,
    w_proj: bass.AP,
    b_proj: bass.AP,
    w_router: bass.AP,
    w1: bass.AP,
    b1: bass.AP,
    w_out: bass.AP,
    b_out: bass.AP,
    gamma: bass.AP,
    beta: bass.AP,
    out: bass.AP,
):
    f32, f16, bf16 = mybir.dt.float32, mybir.dt.float16, mybir.dt.bfloat16
    i32, u32 = mybir.dt.int32, mybir.dt.uint32
    ALU = mybir.AluOpType
    ACT = mybir.ActivationFunctionType
    AX = mybir.AxisListType

    P = 128
    B, T, C = x.shape
    E, _, I = w1.shape
    N = B * T
    HEADS = 16
    HD = C // HEADS
    BLK = 64
    SCALE = float(HD) ** -0.5
    TILES = N // P
    SEQ = T // P
    CC = C // P
    IC = I // P
    SLOT_TILES = TILES + E - 1
    SLOTS = SLOT_TILES * P
    W_UP = 64.0
    W_DOWN = 1.0 / W_UP
    EPS_OUTER, EPS_FFN = 1e-5, 1e-12
    MASKED = -1e30
    ROW = C + 1
    NO_TOKEN = 1 << 20
    UNITS = E * CC
    assert UNITS * 2 == TILES and TILES % 2 == 0 and SLOT_TILES % 2 == 1

    x_rows = x.rearrange("b (t p) c -> (b t) p c", p=P)
    out_rows = out.rearrange("b t c -> (b t) c")
    w1_units = w1.rearrange("e (k p) i -> (e k) p i", p=P)
    slots = nc.dram_tensor("slots", [SLOTS, ROW], f32, kind="Internal").ap()
    slot_tiles = slots.rearrange("(j p) c -> j p c", p=P)

    def wait(eng, sem, count):
        if not isinstance(count, int) or count > 0:
            eng.wait_ge(sem, count)

    ctx = ExitStack()
    with ctx:
        def sb(name, shape, dt):
            return ctx.enter_context(nc.sbuf_tensor(name, shape, dt))

        def sem(name):
            return ctx.enter_context(nc.semaphore(name))

        wa_in = sb("wa_in", [P, CC, 3 * C], f32)
        wp_in = sb("wp_in", [P, CC, C], f32)
        wo_in = sb("wo_in", [P, IC, C], f32)
        bqk_in = sb("bqk_in", [1, 2 * C], f32)
        wa = [sb(f"wa_{s}", [P, CC, 3 * C], f16) for s in ("hi", "lo")]
        wp = [sb(f"wp_{s}", [P, CC, C], f16) for s in ("hi", "lo")]
        wo = [sb(f"wo_{s}", [P, IC, C], f16) for s in ("hi", "lo")]
        w1s = [sb(f"w1_{s}", [P, UNITS, I], f16) for s in ("hi", "lo")]
        w1_in = sb("w1_in", [P, I], f32)
        bqk = sb("bqk", [64, 2 * C], f16)
        ones16 = sb("ones16", [64, P], f16)
        bv = sb("bv", [P, C], f32)
        bp = sb("bp", [P, C], f32)
        bo = sb("bo", [P, C], f32)
        gam = sb("gam", [P, C], f32)
        bet = sb("bet", [P, C], f32)
        wr_in = sb("wr_in", [E, C], f32)
        wrT = sb("wrT", [P, CC, E], f32)
        b1_in = sb("b1_in", [E * IC, P], f32)
        b1T = sb("b1T", [P, E * IC], f32)
        ident = sb("ident", [P, P], f32)
        ident_b = sb("ident_b", [P, P], bf16)
        eye64 = sb("eye64", [P, BLK], bf16)
        mask_q = sb("mask_q", [P, 2, 4, P], bf16)
        mask_k = sb("mask_k", [P, 3, P], bf16)
        band = sb("band", [P, 8], f32)
        evod = sb("evod", [P, 2], f32)
        before = sb("before", [P, P], bf16)
        ones_b = sb("ones_b", [P, P], bf16)
        fill = sb("fill", [P, ROW], f32)
        power, zero, eps_outer, eps_ffn = (sb(n, [P, 1], f32) for n in ("power", "zero", "eps_outer", "eps_ffn"))

        xin = [sb(f"xin{k}", [P, C], f32) for k in range(2)]
        xres = [sb(f"xres{k}", [P, C], f32) for k in range(2)]
        xT = [sb(f"xT_{s}", [P, CC, P], f16) for s in ("hi", "lo")]
        q = [sb(f"q{k}", [P, 2, CC, P], f16) for k in range(2)]
        k_ = [sb(f"k{k}", [P, 4, CC, BLK + P], f16) for k in range(2)]
        v_cur = [sb(f"v_cur{k}", [P, HEADS, HD + 1], f32) for k in range(2)]
        v_mid = [sb(f"v_mid{k}", [P, HEADS, HD + 1], f32) for k in range(2)]
        mx = [sb(f"mx{k}", [P, 8], f32) for k in range(2)]
        diag = [sb(f"diag{k}", [P, 2, 8, BLK], bf16) for k in range(2)]
        probs = [sb(f"probs{k}", [P, 2, 2, 4 * BLK], f32) for k in range(2)]
        rden = sb("rden", [P, HEADS], f32)
        att = sb("att", [P, HEADS, HD], f32)
        attT = [sb(f"attT_{s}", [P, CC, P], f16) for s in ("hi", "lo")]
        y = sb("y", [P, C], f32)
        stats = sb("stats", [P, 6], f32)
        meanvar = sb("meanvar", [P, 2], f32)
        veps = sb("veps", [P, 1], f32)
        rstd = sb("rstd", [P, 1], f32)
        x1 = sb("x1", [P, C], f32)
        x1T = sb("x1T", [P, CC, P], f32)
        rows = sb("rows", [P, TILES, ROW], f32)
        logits = sb("logits", [P, TILES, E], f32)

        slab = [t[:, :, :, :].rearrange("p g b c -> p (g b c)")[:, n * TILES * E:(n + 1) * TILES * E]
                for t in probs for n in range(4)]
        desc = sb("desc", [P, E], f32)
        top = sb("top", [P, TILES], f32)
        hit = slab[0].rearrange("p (t e) -> p t e", e=E)
        pick = slab[1].rearrange("p (t e) -> p t e", e=E)
        first = sb("first", [P, TILES], f32)
        onehot = sb("onehot", [P, TILES, E], bf16)
        in_tile = slab[4].rearrange("p (e t) -> p e t", e=E)
        ones_et = sb("ones_et", [P, E * TILES], f32)
        upto = sb("upto", [P, E * TILES], f32)
        ahead = slab[5].rearrange("p (e t) -> p e t", e=E)
        total = sb("total", [P, E], f32)
        thresholds = sb("thresholds", [P, E, TILES], f32)
        over = slab[6].rearrange("p (e t) -> p e t", e=E)
        ntiles = sb("ntiles", [P, E], f32)
        tend = sb("tend", [P, E], f32)
        tstart = sb("tstart", [P, E], f32)
        shift = sb("shift", [P, E], f32)
        place = slab[7].rearrange("p (e t) -> p e t", e=E)
        place2 = slab[2].rearrange("p (t e) -> p t e", e=E)
        place3 = slab[3].rearrange("p (t e) -> p t e", e=E)
        slot_f = sb("slot_f", [P, TILES], f32)
        slot_of = sb("slot_of", [P, TILES], i32)
        tile_no = sb("tile_no", [1, SLOT_TILES, E - 1], f32)
        past = sb("past", [1, SLOT_TILES, E - 1], f32)
        expert_f = sb("expert_f", [1, SLOT_TILES], f32)
        expert = sb("expert", [1, SLOT_TILES], i32)

        xa = [sb(f"xa{k}", [P, C], f32) for k in range(2)]
        xr = [sb(f"xr{k}", [P, ROW], f32) for k in range(2)]
        sT = [[sb(f"sT{k}_{s}", [P, CC, P], f16) for s in ("hi", "lo")] for k in range(2)]
        free = rows[:, :, :].rearrange("p t c -> p (t c)")
        g = [free[:, k * I:(k + 1) * I].rearrange("p (i t) -> p i t", i=IC) for k in range(2)]
        h = [[free[:, 2 * I + n * (I // 2):2 * I + (n + 1) * (I // 2)].bitcast(f16)
              .rearrange("p (i t) -> p i t", i=IC) for n in (2 * k, 2 * k + 1)] for k in range(2)]
        xbo = [sb(f"xbo{k}", [P, C], f32) for k in range(2)]
        xbe = [sb(f"xbe{k}", [P, C], f32) for k in range(2)]
        y2 = sb("y2", [P, C], f32)
        n1 = sb("n1", [P, C], f32)
        ng = sb("ng", [P, C], f32)
        z = sb("z", [P, C], f32)
        stats_a = sb("stats_a", [P, 6], f32)
        stats_b = sb("stats_b", [P, 6], f32)
        mv_a = sb("mv_a", [P, 2], f32)
        mv_b = sb("mv_b", [P, 2], f32)
        ve_a = sb("ve_a", [P, 1], f32)
        ve_b = sb("ve_b", [P, 1], f32)
        rs_a = sb("rs_a", [P, 1], f32)
        rs_b = sb("rs_b", [P, 1], f32)
        fin = [sb(f"fin{k}", [P, C], f32) for k in range(2)]

        ps = ctx.enter_context(nc.psum_tensor("ps", [P, 8, 512], f32))
        ps_x = ps[:, 0, 0:CC * P].rearrange("p (k t) -> p k t", k=CC)
        ps_qk = ps[:, 1, :].rearrange("p (m t) -> p m t", m=4)
        ps_m = ps[:, 2, :]
        ps_s = ps[:, 3:5, :]
        ps_t = ps[:, 5:7, :]
        ps_o = ps[:, 7, 0:HEADS * (HD + 1)].rearrange("p (h d) -> p h d", h=HEADS)
        ps_h = [ps[:, 2 * k:2 * k + 2, :] for k in range(2)]
        ps_y = [ps[:, 4 + k, 0:C] for k in range(2)]
        ps_sx = [ps[:, 6 + k, 0:CC * P].rearrange("p (k t) -> p k t", k=CC) for k in range(2)]

        attn_w_ld, ffn_w_ld = sem("attn_w_ld"), sem("ffn_w_ld")
        xin_ld = [sem(f"xin_ld{k}") for k in range(2)]
        xres_ld = [sem(f"xres_ld{k}") for k in range(2)]
        w1_ld, fill_st, disp_st = sem("w1_ld"), sem("fill_st"), sem("disp_st")
        consts_done, consts_step = sem("consts_done"), sem("consts_step")
        evod_done = sem("evod_done")
        whi_done, wlo_done = sem("whi_done"), sem("wlo_done")
        setupT_done, setupT_out = sem("setupT_done"), sem("setupT_out")
        xT_done, xh_done, xl_done = sem("xT_done"), sem("xh_done"), sem("xl_done")
        qk_done, qkh_done, qkl_done = sem("qk_done"), sem("qkh_done"), sem("qkl_done")
        kcar_done = sem("kcar_done")
        v_done, v_out, vlow_done, vhigh_done = sem("v_done"), sem("v_out"), sem("vlow_done"), sem("vhigh_done")
        s_done, mx_done, diaglow_done, diag_done, st_done = sem("s_done"), sem("mx_done"), sem("diaglow_done"), sem("diag_done"), sem("st_done")
        exp_done, pv_done = sem("exp_done"), sem("pv_done")
        rden_done, att_done, attT_done = sem("rden_done"), sem("att_done"), sem("attT_done")
        ah_done, al_done = sem("ah_done"), sem("al_done")
        proj_done, xrb_done, y_done = sem("proj_done"), sem("xrb_done"), sem("y_done")
        bn_done, mv_done, rstd_done = sem("bn_done"), sem("mv_done"), sem("rstd_done")
        x1_done, row_done, x1T_done, x1T_out = sem("x1_done"), sem("row_done"), sem("x1T_done"), sem("x1T_out")
        lg_done, lg_out = sem("lg_done"), sem("lg_out")
        w1h_done, w1l_done = sem("w1h_done"), sem("w1l_done")
        route_step, onehot_done, rank_done = sem("route_step"), sem("onehot_done"), sem("rank_done")
        slots_known = sem("slots_known")
        xa_ld = [sem(f"xa_ld{k}") for k in range(2)]
        xr_ld = [sem(f"xr_ld{k}") for k in range(2)]
        sT_done, sh_done, sl_done = sem("sT_done"), sem("sh_done"), sem("sl_done")
        h_done, g_done, hh_done, hl_done = sem("h_done"), sem("g_done"), sem("hh_done"), sem("hl_done")
        ffn_done, y2_done, bna_done, mva_done = sem("ffn_done"), sem("y2_done"), sem("bna_done"), sem("mva_done")
        rsa_done, n1_done, ng_done, z_done = sem("rsa_done"), sem("n1_done"), sem("ng_done"), sem("z_done")
        bnb_done, mvb_done, rsb_done, fin_done = sem("bnb_done"), sem("mvb_done"), sem("rsb_done"), sem("fin_done")
        veps_done, vea_done, veb_done = sem("veps_done"), sem("vea_done"), sem("veb_done")
        xbo_done, xbe_done = sem("xbo_done"), sem("xbe_done")
        out_st = [sem(f"out_st{k}") for k in range(2)]

        ATTN_LOADS, FFN_LOADS = 5, 6
        N_CONSTS = 1

        def apart(eng):
            eng.wait_ge(attn_w_ld, 16 * ATTN_LOADS)

        def variant(t):
            if isinstance(t, int):
                return min(t % SEQ, 1)
            return (t % SEQ + (SEQ - 1)) // SEQ

        def walk_tokens(eng, body):
            body(-1, 1, -1, True, False, False)
            body(0, 0, 0, True, True, False)
            body(1, 1, 0, True, True, True)
            body(2, 0, 1, True, True, True)
            with eng.Fori(0, (TILES - 4) // 2) as i:
                body(2 * i + 3, 1, i + 1, True, True, True)
                body(2 * i + 4, 0, i + 2, True, True, True)
            body(TILES - 1, 1, (TILES - 1) // 2, False, True, True)
            body(TILES, 0, TILES // 2, False, False, True)

        def walk_slots(eng, body):
            body(-2, 0, -1, True, False, False, False)
            body(-1, 1, -1, True, True, False, False)
            body(0, 0, 0, True, True, True, False)
            body(1, 1, 0, True, True, True, True)
            body(2, 0, 1, True, True, True, True)
            with eng.Fori(0, (SLOT_TILES - 5) // 2) as i:
                body(2 * i + 3, 1, i + 1, True, True, True, True)
                body(2 * i + 4, 0, i + 2, True, True, True, True)
            last = SLOT_TILES - 1
            body(last - 1, 1, (last - 1) // 2, False, True, True, True)
            body(last, 0, last // 2, False, False, True, True)
            body(last + 1, 1, (last + 1) // 2, False, False, False, True)

        block = ctx.enter_context(nc.Block())

        @block.sync
        def _(sp):
            sp.dma_start(xin[0][:, :], x_rows[0]).then_inc(xin_ld[0], 16)
            sp.dma_start(wa_in[:, :, :], w_attn.rearrange("(k p) n -> p k n", p=P)).then_inc(attn_w_ld, 16)
            sp.dma_start(xin[1][:, :], x_rows[1]).then_inc(xin_ld[1], 16)
            sp.dma_start(bqk_in[:, :], b_attn[0:2 * C].unsqueeze(0)).then_inc(attn_w_ld, 16)
            sp.dma_start(bv[:, :], b_attn[2 * C:3 * C].unsqueeze(0).broadcast_to([P, C])).then_inc(attn_w_ld, 16)
            sp.dma_start(wp_in[:, :, :], w_proj.rearrange("(k p) n -> p k n", p=P)).then_inc(attn_w_ld, 16)
            sp.dma_start(bp[:, :], b_proj.unsqueeze(0).broadcast_to([P, C])).then_inc(attn_w_ld, 16)

            sp.wait_ge(consts_done, N_CONSTS)
            sp.dma_start(slot_tiles.rearrange("j p c -> p j c"),
                         fill[:, :].unsqueeze(1).broadcast_to([P, SLOT_TILES, ROW])).then_inc(fill_st, 16)

            def body(t, p, hf):
                if not isinstance(t, int) or t + 2 < TILES:
                    wait(sp, xT_done, t + 1)
                    sp.dma_start(xin[p][:, :], x_rows[t + 2]).then_inc(xin_ld[p], 16)
                wait(sp, y_done, t - 1)
                sp.dma_start(xres[p][:, :], x_rows[t]).then_inc(xres_ld[p], 16)
                if p == 0:
                    wait(sp, w1l_done, hf)
                    sp.dma_start(w1_in[:, :], w1_units[hf]).then_inc(w1_ld, 16)

            for t in range(3):
                body(t, t % 2, t // 2)
            with sp.Fori(0, (TILES - 6) // 2) as i:
                body(2 * i + 3, 1, i + 1)
                body(2 * i + 4, 0, i + 2)
            for t in range(TILES - 3, TILES):
                body(t, t % 2, t // 2)

            sp.wait_ge(fill_st, 16)
            sp.wait_ge(disp_st, 16 * TILES)
            sp.dma_start(xa[0][:, :], slot_tiles[0][:, 0:C]).then_inc(xa_ld[0], 16)
            sp.dma_start(xa[1][:, :], slot_tiles[1][:, 0:C]).then_inc(xa_ld[1], 16)
            sp.wait_ge(sT_done, 1)
            sp.dma_start(xa[0][:, :], slot_tiles[2][:, 0:C]).then_inc(xa_ld[0], 16)

            def loads(j, p, hf):
                if not isinstance(j, int) or j + 3 < SLOT_TILES:
                    sp.wait_ge(sT_done, j + 2)
                    sp.dma_start(xa[1 - p][:, :], slot_tiles[j + 3][:, 0:C]).then_inc(xa_ld[1 - p], 16)
                wait(sp, out_st[p], 16 * hf)
                sp.dma_start(xr[p][:, :], slot_tiles[j]).then_inc(xr_ld[p], 16)

            for j in range(3):
                loads(j, j % 2, j // 2)
            with sp.Fori(0, (SLOT_TILES - 7) // 2) as i:
                loads(2 * i + 3, 1, i + 1)
                loads(2 * i + 4, 0, i + 2)
            for j in range(SLOT_TILES - 4, SLOT_TILES):
                loads(j, j % 2, j // 2)
            sp.wait_ge(out_st[0], 16 * ((SLOT_TILES + 1) // 2))
            sp.wait_ge(out_st[1], 16 * (SLOT_TILES // 2))

        @block.gpsimd
        def _(pool):
            step = [0]

            def link(ins):
                step[0] += 1
                ins.then_inc(consts_step, 1)
                pool.wait_ge(consts_step, step[0])

            link(nc.gpsimd.memset(ident[:, :], 0.0))
            link(nc.gpsimd.affine_select(out=ident[:, :], in_=ident[:, :], compare_op=ALU.not_equal, fill=1.0,
                                         base=0, pattern=[[-1, P]], channel_multiplier=1))
            nc.gpsimd.tensor_copy(ident_b[:, :], ident[:, :])
            link(nc.gpsimd.tensor_tensor(eye64[:, :], ident[:, 0:BLK], ident[:, BLK:P], ALU.add))
            link(nc.gpsimd.memset(fill[:, :], 0.0))
            link(nc.gpsimd.memset(fill[:, C:ROW].bitcast(i32), NO_TOKEN))
            link(nc.gpsimd.memset(band[:, :], W_DOWN))
            link(nc.gpsimd.affine_select(out=band[:, :], in_=band[:, :], compare_op=ALU.is_ge, fill=0.0,
                                         base=0, pattern=[[-HD, 8]], channel_multiplier=1))
            link(nc.gpsimd.affine_select(out=band[:, :], in_=band[:, :], compare_op=ALU.is_ge, fill=0.0,
                                         base=HD - 1, pattern=[[HD, 8]], channel_multiplier=-1))
            nc.gpsimd.memset(bqk[:, :], 0.0)
            nc.gpsimd.memset(ones16[:, :], 1.0)
            link(nc.gpsimd.memset(mask_q[:, :, :, :], 0.0))
            for b in range(2):
                r = slice(BLK * b, BLK * b + BLK)
                for sign, base in ((1, 0), (-1, BLK)):
                    link(nc.gpsimd.affine_select(
                        out=mask_q[r, :, :, :], in_=mask_q[r, :, :, :], compare_op=ALU.is_ge, fill=MASKED,
                        base=base, pattern=[[0, 2], [0, 4], [sign, P]], channel_multiplier=-sign))
            link(nc.gpsimd.memset(mask_q[0:BLK, 0, :, 0:BLK], MASKED))
            link(nc.gpsimd.memset(mask_k[:, :, :], -1.0))
            for var in range(2):
                link(nc.gpsimd.tensor_copy(mask_k[BLK:P, var, :], mask_q[0:BLK, var, 0, :]))
            link(nc.gpsimd.tensor_copy(mask_k[0:BLK, 2, :], mask_q[BLK:P, 1, 0, :]))
            for half in range(2):
                for b in range(2):
                    r = slice(BLK * (1 - b), BLK * (1 - b) + BLK)
                    link(nc.gpsimd.tensor_copy(diag[half][r, b, :, :],
                                               eye64[r, :].unsqueeze(1).broadcast_to([BLK, 8, BLK])))
            for k in range(2):
                nc.gpsimd.memset(v_cur[k][:, :, :], 1.0)
                nc.gpsimd.memset(v_mid[k][:, :, :], 1.0)
            nc.gpsimd.memset(k_[0][:, :, :, 0:BLK], 0.0)
            link(nc.gpsimd.memset(ones_b[:, :], 1.0))
            link(nc.gpsimd.affine_select(out=before[:, :], in_=ones_b[:, :], compare_op=ALU.is_ge, fill=0.0,
                                         base=-1, pattern=[[1, P]], channel_multiplier=-1))
            nc.gpsimd.iota(rows[:, :, C:ROW].bitcast(i32), pattern=[[P, TILES], [0, 1]], base=0,
                           channel_multiplier=1)
            nc.gpsimd.iota(desc[:, :], pattern=[[-1, E]], base=E, channel_multiplier=0,
                           allow_small_or_imprecise_dtypes=True)
            nc.gpsimd.memset(ones_et[:, :], 1.0)
            for const, value in ((power, -0.5), (zero, 0.0), (eps_outer, EPS_OUTER), (eps_ffn, EPS_FFN)):
                nc.gpsimd.memset(const[:, :], value)
            nc.gpsimd.iota(thresholds[:, :, :], pattern=[[0, E], [P, TILES]], base=0, channel_multiplier=0,
                           allow_small_or_imprecise_dtypes=True)
            nc.gpsimd.iota(tile_no[:, :, :], pattern=[[1, SLOT_TILES], [0, E - 1]], base=0,
                           channel_multiplier=0, allow_small_or_imprecise_dtypes=True).then_inc(consts_done, 1)

            pool.wait_ge(attn_w_ld, 16 * ATTN_LOADS)

            def body(t, p, hf, nxt, cur, prv):
                if cur:
                    pool.wait_ge(qkl_done, t + 1)
                    wait(pool, st_done, 2 * t)
                    nc.gpsimd.tensor_tensor(k_[1 - p][:, :, :, 0:BLK], k_[p][:, :, :, P:P + BLK],
                                            zero[:, :].unsqueeze(2).unsqueeze(3).broadcast_to([P, 4, CC, BLK]),
                                            ALU.add)\
                        .then_inc(kcar_done, 1)
                if prv:
                    pool.wait_ge(xres_ld[1 - p], 16 * (hf + p))
                    nc.gpsimd.tensor_tensor(xres[1 - p][:, :], xres[1 - p][:, :], bp[:, :], ALU.add)\
                        .then_inc(xrb_done, 1)
                if cur:
                    for half in range(2):
                        pool.wait_ge(mx_done, 2 * t + half + 1)
                        wait(pool, st_done, 2 * t - 1 + half)
                        wait(pool, diag_done, 2 * t + half)
                        for b in range(2):
                            r = slice(BLK * b, BLK * b + BLK)
                            if b == 1:
                                pool.wait_ge(diaglow_done, 2 * t + half + 1)
                            nc.gpsimd.tensor_tensor(
                                diag[half][r, b, :, :], eye64[r, :].unsqueeze(1).broadcast_to([BLK, 8, BLK]),
                                mx[half][r, :].unsqueeze(2).broadcast_to([BLK, 8, BLK]), ALU.mult)\
                                .then_inc(diag_done if b else diaglow_done, 1)
                    pool.wait_ge(diag_done, 2 * t + 2)
                if prv:
                    pool.wait_ge(mv_done, t)
                    wait(pool, x1_done, t - 1)
                    nc.gpsimd.tensor_tensor(veps[:, :], meanvar[:, 1:2], eps_outer[:, :], ALU.add)\
                        .then_inc(veps_done, 1)
                    pool.wait_ge(veps_done, t)
                    nc.gpsimd.tensor_tensor(rstd[:, :], veps[:, :], power[:, :], ALU.pow).then_inc(rstd_done, 1)
                    apart(pool)
                    pool.wait_ge(x1_done, t)
                    nc.gpsimd.tensor_copy(rows[:, t - 1, 0:C], x1[:, :]).then_inc(row_done, 1)

            walk_tokens(pool, body)

            pool.wait_ge(row_done, TILES)
            pool.wait_ge(fill_st, 16)
            pool.wait_ge(slots_known, 1)
            for t in range(TILES):
                nc.gpsimd.indirect_dma_start(
                    out=slots, out_offset=bass.IndirectOffsetOnAxis(ap=slot_of[:, t:t + 1], axis=0),
                    in_=rows[:, t, :], in_offset=None, bounds_check=SLOTS - 1, oob_is_err=False)\
                    .then_inc(disp_st, 16)
            pool.wait_ge(ffn_w_ld, 16 * FFN_LOADS)

            def body3(j, p, hf, load, up, down, norm):
                if norm:
                    pool.wait_ge(mva_done, j)
                    wait(pool, n1_done, j - 1)
                    nc.gpsimd.tensor_tensor(ve_a[:, :], mv_a[:, 1:2], eps_ffn[:, :], ALU.add)\
                        .then_inc(vea_done, 1)
                    pool.wait_ge(vea_done, j)
                    nc.gpsimd.tensor_tensor(rs_a[:, :], ve_a[:, :], power[:, :], ALU.pow)\
                        .then_inc(rsa_done, 1)
                if up:
                    pool.wait_ge(g_done, 2 * j + 3)
                    wait(pool, ffn_done, j)
                    nc.gpsimd.tensor_tensor(h[1 - p][0][:, 0:IC // 2, :], g[1 - p][:, 0:IC // 2, :],
                                            zero[:, :].unsqueeze(2).broadcast_to([P, IC // 2, P]), ALU.add)\
                        .then_inc(hh_done, 1)
                if norm:
                    pool.wait_ge(n1_done, j)
                    wait(pool, z_done, j - 1)
                    nc.gpsimd.tensor_tensor(ng[:, :], n1[:, :], gam[:, :], ALU.mult).then_inc(ng_done, 1)
                    pool.wait_ge(ng_done, j)
                    wait(pool, fin_done, j - 1)
                    nc.gpsimd.tensor_tensor(z[:, :], ng[:, :], xbe[1 - p][:, :], ALU.add).then_inc(z_done, 1)
                if up:
                    pool.wait_ge(g_done, 2 * j + 4)
                    nc.gpsimd.tensor_tensor(h[1 - p][0][:, IC // 2:IC, :], g[1 - p][:, IC // 2:IC, :],
                                            zero[:, :].unsqueeze(2).broadcast_to([P, IC // 2, P]), ALU.add)\
                        .then_inc(hh_done, 1)
                if norm:
                    pool.wait_ge(mvb_done, j)
                    wait(pool, fin_done, j - 1)
                    nc.gpsimd.tensor_tensor(ve_b[:, :], mv_b[:, 1:2], eps_outer[:, :], ALU.add)\
                        .then_inc(veb_done, 1)
                    pool.wait_ge(veb_done, j)
                    nc.gpsimd.tensor_tensor(rs_b[:, :], ve_b[:, :], power[:, :], ALU.pow)\
                        .then_inc(rsb_done, 1)
                if down:
                    pool.wait_ge(xr_ld[p], 16 * (hf + 1))
                    wait(pool, y2_done, j - 1)
                    nc.gpsimd.tensor_tensor(xbo[p][:, :], xr[p][:, 0:C], bo[:, :], ALU.add).then_inc(xbo_done, 1)
                    wait(pool, z_done, j - 1)
                    nc.gpsimd.tensor_tensor(xbe[p][:, :], xr[p][:, 0:C], bet[:, :], ALU.add).then_inc(xbe_done, 1)
                if norm:
                    apart(pool)
                    pool.wait_ge(fin_done, j)
                    nc.gpsimd.indirect_dma_start(
                        out=out_rows,
                        out_offset=bass.IndirectOffsetOnAxis(ap=xr[1 - p][:, C:ROW].bitcast(i32), axis=0),
                        in_=fin[1 - p][:, :], in_offset=None, bounds_check=N - 1, oob_is_err=False)\
                        .then_inc(out_st[1 - p], 16)

            walk_slots(pool, body3)

        @block.scalar
        def _(act):
            for dst, src in ((wr_in[:, :], w_router), (b1_in[:, :], b1.rearrange("e (k p) -> (e k) p", p=P)),
                             (wo_in[:, :, :], w_out.rearrange("(k p) n -> p k n", p=P)),
                             (bo[:, :], b_out.unsqueeze(0).broadcast_to([P, C])),
                             (gam[:, :], gamma.unsqueeze(0).broadcast_to([P, C])),
                             (bet[:, :], beta.unsqueeze(0).broadcast_to([P, C]))):
                act.dma_start(dst, src).then_inc(ffn_w_ld, 16)
            act.wait_ge(attn_w_ld, 16 * ATTN_LOADS)
            act.wait_ge(consts_done, N_CONSTS)
            nc.scalar.activation(wa[0][:, :, :], wa_in[:, :, :], ACT.Copy, scale=W_UP).then_inc(whi_done, 1)
            nc.scalar.activation(bqk[0:1, :], bqk_in[:, :], ACT.Copy, scale=W_UP).then_inc(whi_done, 1)
            nc.scalar.activation(wp[0][:, :, :], wp_in[:, :, :], ACT.Copy, scale=W_UP).then_inc(whi_done, 1)
            act.wait_ge(ffn_w_ld, 16 * FFN_LOADS)
            nc.scalar.activation(wo[0][:, :, :], wo_in[:, :, :], ACT.Copy, scale=W_UP).then_inc(whi_done, 1)
            act.wait_ge(setupT_done, 1)
            nc.scalar.activation(wrT[:, :, :], ps[:, 1, 0:CC * E].rearrange("p (k e) -> p k e", k=CC), ACT.Copy)
            nc.scalar.activation(b1T[:, :], ps[:, 1, P:P + E * IC], ACT.Copy).then_inc(setupT_out, 1)
            act.wait_ge(evod_done, 1)

            def body(t, p, hf, nxt, cur, prv):
                if nxt:
                    act.wait_ge(xT_done, t + 2)
                    wait(act, v_done, t + 1)
                    nc.scalar.activation(xT[0][:, :, :], ps_x, ACT.Copy).then_inc(xh_done, 1)
                if prv:
                    act.wait_ge(attT_done, t)
                    wait(act, proj_done, t - 1)
                    nc.scalar.activation(attT[0][:, :, :], ps_m[:, 0:C].rearrange("p (k t) -> p k t", k=CC),
                                         ACT.Copy).then_inc(ah_done, 1)

                def exps(half):
                    act.wait_ge(st_done, 2 * t + half + 1)
                    wait(act, pv_done, 2 * t - 1 + half)
                    nc.scalar.activation(probs[half][:, :, :, :],
                                         ps_t.rearrange("p g (b c) -> p g b c", b=2), ACT.Exp, scale=SCALE)\
                        .then_inc(exp_done, 1)

                if cur:
                    exps(0)
                if nxt:
                    act.wait_ge(qk_done, t + 2)
                    wait(act, st_done, 2 * t)
                    wait(act, kcar_done, t)
                    nc.scalar.activation(q[1 - p][:, 0, :, :], ps_qk[:, 0:2, :], ACT.Copy, scale=W_DOWN)
                    for odd in range(2):
                        last = nc.scalar.activation(k_[1 - p][:, odd, :, BLK:BLK + P], ps_qk[:, 2:4, :],
                                                    ACT.Copy, scale=evod[:, odd:odd + 1])
                    last.then_inc(qkh_done, 1)
                if cur:
                    act.wait_ge(v_out, t + 1)
                    wait(act, pv_done, 2 * t)
                    nc.scalar.activation(v_mid[1 - p][0:BLK, :, 0:HD], v_cur[p][BLK:P, :, 0:HD], ACT.Copy)\
                        .then_inc(vlow_done, 1)
                    exps(1)
                if nxt:
                    act.wait_ge(v_out, t + 2)
                    nc.scalar.activation(v_mid[1 - p][BLK:P, :, 0:HD], v_cur[1 - p][0:BLK, :, 0:HD], ACT.Copy)\
                        .then_inc(vhigh_done, 1)
                if prv:
                    act.wait_ge(x1T_done, t)
                    wait(act, lg_done, t - 1)
                    nc.scalar.activation(x1T[:, :, :], ps_x, ACT.Copy).then_inc(x1T_out, 1)
                    if p == 1:
                        act.wait_ge(w1_ld, 16 * (hf + 1))
                        nc.scalar.activation(w1s[0][:, hf, :], w1_in[:, :], ACT.Copy, scale=W_UP)\
                            .then_inc(w1h_done, 1)
                    act.wait_ge(lg_done, t)
                    nc.scalar.activation(logits[:, t - 1, :], ps_m[:, 0:E], ACT.Copy).then_inc(lg_out, 1)

            walk_tokens(act, body)

            def body3(j, p, hf, load, up, down, norm):
                if up:
                    e = act.value_load(expert[0:1, bass.ds(j + 1, 1)], min_val=0, max_val=E - 1)
                    wait(act, hl_done, 2 * j)
                    for half in range(2):
                        act.wait_ge(h_done, 2 * j + 3 + half)
                        for ic in range(half * IC // 2, (half + 1) * IC // 2):
                            col = (ic % (IC // 2)) * P
                            last = nc.scalar.activation(
                                g[1 - p][:, ic, :], ps_h[1 - p][:, half, col:col + P], ACT.Gelu,
                                bias=b1T[:, bass.ds(e * IC + ic, 1)], scale=W_DOWN)
                        last.then_inc(g_done, 1)
                if load:
                    act.wait_ge(sT_done, j + 3)
                    wait(act, h_done, 2 * j + 2)
                    nc.scalar.activation(sT[p][0][:, :, :], ps_sx[p], ACT.Copy).then_inc(sh_done, 1)

            act.wait_ge(slots_known, 1)
            walk_slots(act, body3)

        @block.vector
        def _(dve):
            dve.wait_ge(consts_done, N_CONSTS)
            nc.vector.tensor_reduce(evod[:, :], band[:, :].rearrange("p (n o) -> p o n", o=2), AX.X, ALU.add)\
                .then_inc(evod_done, 1)
            dve.wait_ge(whi_done, 1)
            nc.vector.scalar_tensor_tensor(wa[1][:, :, :], wa_in[:, :, :], W_UP, wa[0][:, :, :],
                                           ALU.mult, ALU.subtract).then_inc(wlo_done, 1)
            dve.wait_ge(whi_done, 2)
            nc.vector.scalar_tensor_tensor(bqk[32:33, :], bqk_in[:, :], W_UP, bqk[0:1, :],
                                           ALU.mult, ALU.subtract).then_inc(wlo_done, 1)
            dve.wait_ge(whi_done, 3)
            nc.vector.scalar_tensor_tensor(wp[1][:, :, :], wp_in[:, :, :], W_UP, wp[0][:, :, :],
                                           ALU.mult, ALU.subtract).then_inc(wlo_done, 1)
            dve.wait_ge(whi_done, 4)
            nc.vector.scalar_tensor_tensor(wo[1][:, :, :], wo_in[:, :, :], W_UP, wo[0][:, :, :],
                                           ALU.mult, ALU.subtract).then_inc(wlo_done, 1)

            def body(t, p, hf, nxt, cur, prv):
                def maxima(half):
                    dve.wait_ge(s_done, 2 * t + half + 1)
                    wait(dve, diag_done, 2 * t - 1 + half)
                    nc.vector.tensor_reduce(mx[half][:, :], ps_s.rearrange("p g (h k) -> p (g h) k", k=P),
                                            AX.X, ALU.max).then_inc(mx_done, 1)

                if prv:
                    dve.wait_ge(pv_done, 2 * t)
                    wait(dve, att_done, t - 1)
                    nc.vector.reciprocal(rden[:, :], ps_o[:, :, HD]).then_inc(rden_done, 1)
                    dve.wait_ge(rden_done, t)
                    wait(dve, attT_done, t - 1)
                    nc.vector.tensor_tensor(att[:, :, :], ps_o[:, :, 0:HD],
                                            rden[:, :].unsqueeze(2).broadcast_to([P, HEADS, HD]), ALU.mult)\
                        .then_inc(att_done, 1)
                if cur:
                    maxima(0)
                if nxt:
                    dve.wait_ge(xh_done, t + 2)
                    wait(dve, v_done, t + 1)
                    nc.vector.tensor_tensor(xT[1][:, :, :], ps_x, xT[0][:, :, :], ALU.subtract)\
                        .then_inc(xl_done, 1)
                if prv:
                    dve.wait_ge(ah_done, t)
                    wait(dve, proj_done, t - 1)
                    nc.vector.tensor_tensor(attT[1][:, :, :], ps_m[:, 0:C].rearrange("p (k t) -> p k t", k=CC),
                                            attT[0][:, :, :], ALU.subtract).then_inc(al_done, 1)
                if cur:
                    maxima(1)
                if nxt:
                    dve.wait_ge(qkh_done, t + 2)
                    wait(dve, st_done, 2 * t)
                    wait(dve, kcar_done, t)
                    nc.vector.scalar_tensor_tensor(q[1 - p][:, 1, :, :], ps_qk[:, 0:2, :], W_DOWN,
                                                   q[1 - p][:, 0, :, :], ALU.mult, ALU.subtract)
                    for odd in range(2):
                        last = nc.vector.scalar_tensor_tensor(
                            k_[1 - p][:, 2 + odd, :, BLK:BLK + P], ps_qk[:, 2:4, :], evod[:, odd:odd + 1],
                            k_[1 - p][:, odd, :, BLK:BLK + P], ALU.mult, ALU.subtract)
                    last.then_inc(qkl_done, 1)
                if prv:
                    dve.wait_ge(proj_done, t)
                    dve.wait_ge(xrb_done, t)
                    wait(dve, x1_done, t - 1)
                    nc.vector.scalar_tensor_tensor(y[:, :], ps_m[:, 0:C], W_DOWN, xres[1 - p][:, :],
                                                   ALU.mult, ALU.add).then_inc(y_done, 1)
                    dve.wait_ge(y_done, t)
                    nc.vector.bn_stats(stats[:, :], y[:, :]).then_inc(bn_done, 1)
                    apart(dve)
                    dve.wait_ge(bn_done, t)
                    wait(dve, rstd_done, t - 1)
                    nc.vector.bn_aggr(meanvar[:, :], stats[:, :]).then_inc(mv_done, 1)
                if nxt:
                    dve.wait_ge(v_done, t + 2)
                    wait(dve, pv_done, 2 * t)
                    wait(dve, vlow_done, t)
                    wait(dve, vhigh_done, t)
                    nc.vector.scalar_tensor_tensor(
                        v_cur[1 - p][:, :, 0:HD], ps_m[:, 0:C].rearrange("p (h d) -> p h d", h=HEADS), W_DOWN,
                        bv[:, :].rearrange("p (h d) -> p h d", h=HEADS), ALU.mult, ALU.add).then_inc(v_out, 1)
                if prv:
                    dve.wait_ge(rstd_done, t)
                    wait(dve, x1T_done, t - 1)
                    wait(dve, row_done, t - 1)
                    nc.vector.tensor_scalar(x1[:, :], y[:, :], meanvar[:, 0:1], rstd[:, :],
                                            ALU.subtract, ALU.mult).then_inc(x1_done, 1)
                    if p == 1:
                        dve.wait_ge(w1h_done, hf + 1)
                        nc.vector.scalar_tensor_tensor(w1s[1][:, hf, :], w1_in[:, :], W_UP, w1s[0][:, hf, :],
                                                       ALU.mult, ALU.subtract).then_inc(w1l_done, 1)

            walk_tokens(dve, body)

            step = [0]

            def link(ins):
                step[0] += 1
                ins.then_inc(route_step, 1)
                dve.wait_ge(route_step, step[0])

            lg = logits[:, :, :]
            over_e = lambda a: a.unsqueeze(2).broadcast_to([P, TILES, E])
            per_e = desc[:, :].unsqueeze(1).broadcast_to([P, TILES, E])
            dve.wait_ge(lg_out, TILES)
            link(nc.vector.tensor_reduce(top[:, :], lg, AX.X, ALU.max))
            link(nc.vector.tensor_tensor(hit[:, :, :], lg, over_e(top[:, :]), ALU.is_equal))
            link(nc.vector.tensor_tensor(pick[:, :, :], hit[:, :, :], per_e, ALU.mult))
            link(nc.vector.tensor_reduce(first[:, :], pick[:, :, :], AX.X, ALU.max))
            nc.vector.tensor_tensor(onehot[:, :, :], per_e, over_e(first[:, :]), ALU.is_equal)\
                .then_inc(onehot_done, 1)
            dve.wait_ge(rank_done, 1)
            tot_ps = ps[:, 1, 0:TILES * E].rearrange("p (t e) -> p e t", e=E)
            link(nc.vector.tensor_copy(in_tile[:, :, :], tot_ps))
            link(nc.vector.tensor_tensor_scan(upto[:, :], ones_et[:, :], in_tile[:, :, :].rearrange("p e t -> p (e t)"),
                                              0.0, ALU.mult, ALU.add))
            link(nc.vector.tensor_tensor(ahead[:, :, :], upto[:, :].rearrange("p (e t) -> p e t", e=E),
                                         in_tile[:, :, :], ALU.subtract))
            link(nc.vector.tensor_reduce(total[:, :], in_tile[:, :, :], AX.X, ALU.add))
            link(nc.vector.tensor_tensor(over[:, :, :], total[:, :].unsqueeze(2).broadcast_to([P, E, TILES]),
                                         thresholds[:, :, :], ALU.is_gt))
            link(nc.vector.tensor_reduce(ntiles[:, :], over[:, :, :], AX.X, ALU.add))
            link(nc.vector.tensor_tensor_scan(tend[:, :], ones_et[:, 0:E], ntiles[:, :], 0.0, ALU.mult, ALU.add))
            link(nc.vector.tensor_tensor(tstart[:, :], tend[:, :], ntiles[:, :], ALU.subtract))
            link(nc.vector.scalar_tensor_tensor(shift[:, :], tstart[:, :], float(P), ahead[:, :, 0],
                                                ALU.mult, ALU.subtract))
            link(nc.vector.tensor_tensor(place[:, :, :], ahead[:, :, :],
                                         shift[:, :].unsqueeze(2).broadcast_to([P, E, TILES]), ALU.add))
            link(nc.vector.tensor_tensor(place2[:, :, :], ps[:, 0, 0:TILES * E].rearrange("p (t e) -> p t e", e=E),
                                         place[:, :, :].rearrange("p e t -> p t e"), ALU.add))
            link(nc.vector.tensor_tensor(place3[:, :, :], place2[:, :, :], onehot[:, :, :], ALU.mult))
            link(nc.vector.tensor_reduce(slot_f[:, :], place3[:, :, :], AX.X, ALU.add))
            link(nc.vector.tensor_copy(slot_of[:, :], slot_f[:, :]))
            link(nc.vector.tensor_tensor(past[:, :, :], tile_no[:, :, :],
                                         tend[0:1, 0:E - 1].unsqueeze(1).broadcast_to([1, SLOT_TILES, E - 1]),
                                         ALU.is_ge))
            link(nc.vector.tensor_reduce(expert_f[:, :], past[:, :, :], AX.X, ALU.add))
            nc.vector.tensor_copy(expert[:, :], expert_f[:, :]).then_inc(slots_known, 1)

            def body3(j, p, hf, load, up, down, norm):
                def split(half):
                    a, b = half * IC // 2, (half + 1) * IC // 2
                    dve.wait_ge(hh_done, 2 * j + 3 + half)
                    wait(dve, ffn_done, j)
                    nc.vector.tensor_tensor(h[1 - p][1][:, a:b, :], g[1 - p][:, a:b, :], h[1 - p][0][:, a:b, :],
                                            ALU.subtract).then_inc(hl_done, 1)

                if norm:
                    dve.wait_ge(ffn_done, j)
                    dve.wait_ge(xbo_done, j)
                    wait(dve, n1_done, j - 1)
                    nc.vector.scalar_tensor_tensor(y2[:, :], ps_y[1 - p], W_DOWN, xbo[1 - p][:, :],
                                                   ALU.mult, ALU.add).then_inc(y2_done, 1)
                    dve.wait_ge(y2_done, j)
                    nc.vector.bn_stats(stats_a[:, :], y2[:, :]).then_inc(bna_done, 1)
                    apart(dve)
                    dve.wait_ge(bna_done, j)
                    wait(dve, rsa_done, j - 1)
                    nc.vector.bn_aggr(mv_a[:, :], stats_a[:, :]).then_inc(mva_done, 1)
                if up:
                    split(0)
                if norm:
                    dve.wait_ge(rsa_done, j)
                    wait(dve, ng_done, j - 1)
                    nc.vector.tensor_scalar(n1[:, :], y2[:, :], mv_a[:, 0:1], rs_a[:, :],
                                            ALU.subtract, ALU.mult).then_inc(n1_done, 1)
                if up:
                    split(1)
                if norm:
                    dve.wait_ge(z_done, j)
                    nc.vector.bn_stats(stats_b[:, :], z[:, :]).then_inc(bnb_done, 1)
                    apart(dve)
                    dve.wait_ge(bnb_done, j)
                    wait(dve, rsb_done, j - 1)
                    nc.vector.bn_aggr(mv_b[:, :], stats_b[:, :]).then_inc(mvb_done, 1)
                if load:
                    dve.wait_ge(sh_done, j + 3)
                    wait(dve, h_done, 2 * j + 2)
                    nc.vector.tensor_tensor(sT[p][1][:, :, :], ps_sx[p], sT[p][0][:, :, :], ALU.subtract)\
                        .then_inc(sl_done, 1)
                if norm:
                    dve.wait_ge(rsb_done, j)
                    wait(dve, out_st[1 - p], 16 * (hf + p - 1))
                    nc.vector.tensor_scalar(fin[1 - p][:, :], z[:, :], mv_b[:, 0:1], rs_b[:, :],
                                            ALU.subtract, ALU.mult).then_inc(fin_done, 1)

            walk_slots(dve, body3)

        @block.tensor
        def _(pe):
            mm = nc.tensor.matmul

            def product(dst, left, right, start=True, stop=True):
                terms = [(l, r) for k in range(len(left)) for l, r in
                         ((left[k][0], right[k][0]), (left[k][1], right[k][0]), (left[k][0], right[k][1]))]
                for n, (l, r) in enumerate(terms):
                    last = mm(dst, l, r, start=start and n == 0, stop=stop and n == len(terms) - 1)
                return last

            pe.wait_ge(consts_done, N_CONSTS)
            pe.wait_ge(ffn_w_ld, 16 * FFN_LOADS)
            for k in range(CC):
                nc.tensor.transpose(ps[:, 1, k * E:(k + 1) * E], wr_in[:, k * P:(k + 1) * P], ident[0:E, 0:E])
            nc.tensor.transpose(ps[:, 1, P:P + E * IC], b1_in[:, :], ident[0:E * IC, 0:E * IC])\
                .then_inc(setupT_done, 1)
            pe.wait_ge(setupT_out, 1)

            def body(t, p, hf, nxt, cur, prv):
                var = variant(t) if cur else 0

                def heads(half, gg):
                    grp = 2 * half + gg
                    for ce in range(4):
                        yield ce, ce // 2, ce % 2, 8 * (ce // 2) + 2 * grp + ce % 2, slice(32 * grp, 32 * grp + 32)

                def scores(half):
                    pe.wait_ge(qkl_done, t + 1)
                    wait(pe, kcar_done, t)
                    wait(pe, mx_done, 2 * t + half)
                    for gg in range(2):
                        mm(ps_s[:, gg, :], ident_b[:, :],
                           mask_q[:, bass.ds(var, 1), :, :].rearrange("p a c k -> p (a c k)"),
                           start=True, stop=False, skip_group_check=True)
                    for ce in range(4):
                        for gg in range(2):
                            _, c, odd, _, r = list(heads(half, gg))[ce]
                            for b in range(2):
                                last = mm(ps_s[BLK * b:BLK * b + BLK, gg, ce * P:(ce + 1) * P],
                                          q[p][r, 0, c, BLK * b:BLK * b + BLK],
                                          k_[p][r, odd, c, BLK * b:BLK * b + P],
                                          start=False, stop=ce == 3, skip_group_check=True)
                    last.then_inc(s_done, 1)

                def scores_t(half):
                    wait(pe, exp_done, 2 * t + half)
                    for gg in range(2):
                        for ce, c, odd, _, r in heads(half, gg):
                            for b in range(2):
                                dst = ps_t[:, gg, (4 * b + ce) * BLK:(4 * b + ce + 1) * BLK]
                                for klo, qlo in ((0, 0), (1, 0), (0, 1)):
                                    mm(dst, k_[p][r, 2 * klo + odd, c, BLK * b:BLK * b + P],
                                       q[p][r, qlo, c, BLK * b:BLK * b + BLK],
                                       start=ce == 0 and b == 0 and klo + qlo == 0, stop=False,
                                       skip_group_check=True)

                def less_maxima(half):
                    pe.wait_ge(diag_done, 2 * t + half + 1)
                    for gg in range(2):
                        for b in range(2):
                            left = mask_k[:, bass.ds(var, 1), :].rearrange("p a k -> p (a k)") if b == 0 \
                                else mask_k[:, 2, :]
                            last = mm(ps_t[:, gg, b * 4 * BLK:(b + 1) * 4 * BLK], left,
                                      diag[half][:, b, 4 * gg:4 * gg + 4, :].rearrange("p h q -> p (h q)"),
                                      start=False, stop=True, skip_group_check=True)
                    last.then_inc(st_done, 1)

                def values(half):
                    pe.wait_ge(exp_done, 2 * t + half + 1)
                    pe.wait_ge(vhigh_done, t + 1)
                    wait(pe, vlow_done, t)
                    wait(pe, att_done, t)
                    for gg in range(2):
                        for ce, c, odd, hd, r in heads(half, gg):
                            for b in range(2):
                                last = mm(ps_o[BLK * b:BLK * b + BLK, hd, :],
                                          probs[half][:, gg, b, ce * BLK:(ce + 1) * BLK],
                                          (v_cur if b else v_mid)[p][:, hd, :], start=True, stop=True)
                    last.then_inc(pv_done, 1)

                if cur:
                    scores(0)
                if nxt:
                    pe.wait_ge(xin_ld[1 - p], 16 * (hf + p + 1))
                    wait(pe, x1T_out, t - 1)
                    for k in range(CC):
                        last = nc.tensor.transpose(ps_x[:, k, :], xin[1 - p][:, k * P:(k + 1) * P], ident[:, :])
                    last.then_inc(xT_done, 1)
                if cur:
                    scores_t(0)
                if prv:
                    pe.wait_ge(att_done, t)
                    wait(pe, lg_out, t - 1)
                    for k in range(CC):
                        last = nc.tensor.transpose(ps_m[:, k * P:(k + 1) * P],
                                                   att[:, k * 8:(k + 1) * 8, :].rearrange("p h d -> p (h d)"),
                                                   ident[:, :])
                    last.then_inc(attT_done, 1)
                if cur:
                    scores(1)
                    less_maxima(0)
                if nxt:
                    pe.wait_ge(xl_done, t + 2)
                    wait(pe, qkl_done, t + 1)
                    if isinstance(t, int) and t < 0:
                        pe.wait_ge(wlo_done, 2)
                    for m in range(4):
                        cols = slice(m * P, (m + 1) * P)
                        mm(ps_qk[:, m, :], bqk[:, cols], ones16[:, :], start=True, stop=False)
                        last = product(ps_qk[:, m, :], [(wa[0][:, k, cols], wa[1][:, k, cols]) for k in range(CC)],
                                       [(xT[0][:, k, :], xT[1][:, k, :]) for k in range(CC)], start=False)
                    last.then_inc(qk_done, 1)
                if cur:
                    scores_t(1)
                if prv:
                    pe.wait_ge(al_done, t)
                    if isinstance(t, int):
                        pe.wait_ge(wlo_done, 4)
                    product(ps_m[:, 0:C], [(attT[0][:, k, :], attT[1][:, k, :]) for k in range(CC)],
                            [(wp[0][:, k, :], wp[1][:, k, :]) for k in range(CC)]).then_inc(proj_done, 1)
                if cur:
                    less_maxima(1)
                if nxt:
                    wait(pe, y_done, t)
                    product(ps_m[:, 0:C], [(xT[0][:, k, :], xT[1][:, k, :]) for k in range(CC)],
                            [(wa[0][:, k, 2 * C:3 * C], wa[1][:, k, 2 * C:3 * C]) for k in range(CC)])\
                        .then_inc(v_done, 1)
                if cur:
                    values(0)
                if prv:
                    pe.wait_ge(x1_done, t)
                    wait(pe, xl_done, t + 2 if nxt else 0)
                    for k in range(CC):
                        last = nc.tensor.transpose(ps_x[:, k, :], x1[:, k * P:(k + 1) * P], ident[:, :])
                    last.then_inc(x1T_done, 1)
                if cur:
                    values(1)
                if prv:
                    pe.wait_ge(x1T_out, t)
                    wait(pe, v_out, t + 2 if nxt else 0)
                    for k in range(CC):
                        last = mm(ps_m[:, 0:E], x1T[:, k, :], wrT[:, k, :], start=k == 0, stop=k == CC - 1)
                    last.then_inc(lg_done, 1)

            walk_tokens(pe, body)

            pe.wait_ge(onehot_done, 1)
            oh = onehot[:, :, :].rearrange("p t e -> p (t e)")
            mm(ps[:, 0, 0:TILES * E], before[:, :], oh, start=True, stop=True)
            mm(ps[:, 1, 0:TILES * E], ones_b[:, :], oh, start=True, stop=True).then_inc(rank_done, 1)

            def body3(j, p, hf, load, up, down, norm):
                if up:
                    e = pe.value_load(expert[0:1, bass.ds(j + 1, 1)], min_val=0, max_val=E - 1)
                    pe.wait_ge(sl_done, j + 2)
                    for half in range(2):
                        wait(pe, g_done, 2 * j - 1 + half)
                        for ic in range(half * IC // 2, (half + 1) * IC // 2):
                            col = (ic % (IC // 2)) * P

                            def weights(s, k):
                                return w1s[s][:, bass.ds(e * CC + k, 1), ic * P:(ic + 1) * P]\
                                    .rearrange("p a i -> p (a i)")

                            last = product(ps_h[1 - p][:, half, col:col + P],
                                           [(weights(0, k), weights(1, k)) for k in range(CC)],
                                           [(sT[1 - p][0][:, k, :], sT[1 - p][1][:, k, :]) for k in range(CC)])
                        last.then_inc(h_done, 1)
                if load:
                    pe.wait_ge(xa_ld[p], 16 * (hf + 2))
                    wait(pe, sl_done, j + 1)
                    for k in range(CC):
                        last = nc.tensor.transpose(ps_sx[p][:, k, :], xa[p][:, k * P:(k + 1) * P], ident[:, :])
                    last.then_inc(sT_done, 1)
                if down:
                    wait(pe, y2_done, j - 1)
                    for half in range(2):
                        pe.wait_ge(hl_done, 2 * j + half + 1)
                        ics = range(half * IC // 2, (half + 1) * IC // 2)
                        last = product(ps_y[p], [(h[p][0][:, ic, :], h[p][1][:, ic, :]) for ic in ics],
                                       [(wo[0][:, ic, :], wo[1][:, ic, :]) for ic in ics],
                                       start=half == 0, stop=half == 1)
                    last.then_inc(ffn_done, 1)

            pe.wait_ge(slots_known, 1)
            pe.wait_ge(w1l_done, UNITS)
            walk_slots(pe, body3)


_INS = ['L0_attn_x', 'L0_attn_W_attn', 'L0_attn_b_attn', 'L0_attn_W_proj', 'L0_attn_b_proj', 'L0_ffn_Wr',
        'L0_ffn_W1', 'L0_ffn_b1', 'L0_ffn_Wo', 'L0_ffn_bo', 'L0_ffn_gamma', 'L0_ffn_beta']
_OUTS = [((2, 2048, 256), 'float32')]


def kernel(**inputs):
    import numpy as _np
    import concourse.bacc as _bacc
    from concourse import mybir as _mybir
    from concourse.bass_utils import run_bass_kernel_spmd as _run

    nc = _bacc.Bacc("TRN2", target_bir_lowering=False, num_devices=1)
    arrays, args = {}, []
    for name in _INS:
        a = _np.ascontiguousarray(inputs[name])
        arrays[f"in_{name}_dram"] = a
        args.append(nc.dram_tensor(f"in_{name}_dram", a.shape, _mybir.dt.from_np(a.dtype), kind="ExternalInput").ap())
    for i, (shape, dtype) in enumerate(_OUTS):
        dt = _mybir.dt.from_np(_np.dtype(dtype))
        args.append(nc.dram_tensor(f"out_{i}_dram", shape, dt, kind="ExternalOutput").ap())
    attention_then_routed_ffn(nc, *args)
    r = _run(nc, [arrays], core_ids=[0])
    got = tuple(r.results[0][f"out_{i}_dram"] for i in range(len(_OUTS)))
    return got[0]
```

```python
import concourse.bass as bass
from concourse import mybir
from contextlib import ExitStack


def attention_then_routed_ffn(
    nc: bass.Bass,
    x: bass.AP,
    w_attn: bass.AP,
    b_attn: bass.AP,
    w_proj: bass.AP,
    b_proj: bass.AP,
    w_router: bass.AP,
    w1: bass.AP,
    b1: bass.AP,
    w_out: bass.AP,
    b_out: bass.AP,
    gamma: bass.AP,
    beta: bass.AP,
    out: bass.AP,
):
    f32, f16, bf16 = mybir.dt.float32, mybir.dt.float16, mybir.dt.bfloat16
    i32, u32 = mybir.dt.int32, mybir.dt.uint32
    ALU = mybir.AluOpType
    ACT = mybir.ActivationFunctionType
    AX = mybir.AxisListType

    P = 128
    B, T, C = x.shape
    E, _, I = w1.shape
    N = B * T
    HEADS = 16
    HD = C // HEADS
    BLK = 64
    SCALE = float(HD) ** -0.5
    TILES = N // P
    SEQ = T // P
    CC = C // P
    CH = HEADS // CC
    PAIRS = CH // 2
    UNITS_T = CC * 2
    IC = I // P
    SLOT_TILES = TILES + E - 1
    SLOTS = SLOT_TILES * P
    W_UP = 64.0
    W_DOWN = 1.0 / W_UP
    EPS_OUTER, EPS_FFN = 1e-5, 1e-12
    MASKED = -1e30
    ROW = C + 1
    NO_TOKEN = 1 << 20
    UNITS = E * CC
    assert UNITS * 2 == TILES and TILES % 2 == 0 and SLOT_TILES % 2 == 1

    x_rows = x.rearrange("b (t p) c -> (b t) p c", p=P)
    out_rows = out.rearrange("b t c -> (b t) c")
    w1_units = w1.rearrange("e (k p) i -> (e k) p i", p=P)
    slots = nc.dram_tensor("slots", [SLOTS, ROW], f32, kind="Internal").ap()
    slot_tiles = slots.rearrange("(j p) c -> j p c", p=P)

    def wait(eng, sem, count):
        if not isinstance(count, int) or count > 0:
            eng.wait_ge(sem, count)

    ctx = ExitStack()
    with ctx:
        def sb(name, shape, dt):
            return ctx.enter_context(nc.sbuf_tensor(name, shape, dt))

        def sem(name):
            return ctx.enter_context(nc.semaphore(name))

        wa_in = sb("wa_in", [P, CC, 3 * C], f32)
        wp_in = sb("wp_in", [P, 2, C], f32)
        wo_in = sb("wo_in", [P, IC, C], f32)
        bqk_in = sb("bqk_in", [1, 2 * C], f32)
        wa = [sb(f"wa_{s}", [P, CC, 3 * C], f16) for s in ("hi", "lo")]
        wp = [sb(f"wp_{s}", [P, CC, C], f16) for s in ("hi", "lo")]
        wo = [sb(f"wo_{s}", [P, IC, C], f16) for s in ("hi", "lo")]
        w1s = [sb(f"w1_{s}", [P, UNITS, I], f16) for s in ("hi", "lo")]
        w1_in = sb("w1_in", [P, I], f32)
        bqk = sb("bqk", [64, 2 * C], f16)
        ones16 = sb("ones16", [64, P], f16)
        bv = sb("bv", [P, C], f32)
        bp = sb("bp", [P, C], f32)
        bo = sb("bo", [P, C], f32)
        gam = sb("gam", [P, C], f32)
        bet = sb("bet", [P, C], f32)
        wr_in = sb("wr_in", [E, C], f32)
        wrT = sb("wrT", [P, CC, E], f32)
        b1_in = sb("b1_in", [E * IC, P], f32)
        b1T = sb("b1T", [P, E * IC], f32)
        ident = sb("ident", [P, P], f32)
        ident_b = sb("ident_b", [P, P], bf16)
        mask_q = sb("mask_q", [P, 2, P], bf16)
        minus1 = sb("minus1", [P, P], bf16)
        band = sb("band", [P, CH], f32)
        before = sb("before", [P, P], bf16)
        ones_b = sb("ones_b", [P, P], bf16)
        fill = sb("fill", [P, ROW], f32)
        power, zero, eps_outer, eps_ffn = (sb(n, [P, 1], f32) for n in ("power", "zero", "eps_outer", "eps_ffn"))

        xin = [sb(f"xin{k}", [P, C], f32) for k in range(2)]
        xres = [sb(f"xres{k}", [P, C], f32) for k in range(2)]
        xT = [sb(f"xT_{s}", [P, CC, P], f16) for s in ("hi", "lo")]
        q = sb("q", [P, 2, CC, 2, BLK], f16)
        qbd = [sb(f"qbd{k}", [P, 2, CC, 2, CH, BLK], f16) for k in range(2)]
        k_ = [sb(f"k{k}", [P, 2, CC, BLK + P], f16) for k in range(2)]
        v_cur = [sb(f"v_cur{k}", [P, HEADS, HD + 1], f32) for k in range(2)]
        v_mid = [sb(f"v_mid{k}", [P, HEADS, HD + 1], f32) for k in range(2)]
        mx = [sb(f"mx{k}", [P, PAIRS], f32) for k in range(2)]
        diag = [sb(f"diag{k}", [P, PAIRS, P], bf16) for k in range(2)]
        probs = [sb(f"probs{u}", [P, PAIRS, P], f32) for u in range(UNITS_T)]
        rden = sb("rden", [P, CC, 2 * PAIRS], f32)
        att = sb("att", [P, 2, CC, PAIRS, HD], f32)
        attT = [sb(f"attT_{s}", [P, 2, 2, BLK], f16) for s in ("hi", "lo")]
        y = sb("y", [P, C], f32)
        stats = sb("stats", [P, 6], f32)
        meanvar = sb("meanvar", [P, 2], f32)
        veps = sb("veps", [P, 1], f32)
        rstd = sb("rstd", [P, 1], f32)
        x1 = sb("x1", [P, C], f32)
        x1T = sb("x1T", [P, CC, P], f32)
        rows = sb("rows", [P, TILES, ROW], f32)
        logits = sb("logits", [P, TILES, E], f32)

        slab = [t[:, :, :].rearrange("p a q -> p (a q)")[:, n * TILES * E:(n + 1) * TILES * E]
                for t in probs for n in range(2)]
        desc = sb("desc", [P, E], f32)
        top = sb("top", [P, TILES], f32)
        hit = slab[0].rearrange("p (t e) -> p t e", e=E)
        pick = slab[1].rearrange("p (t e) -> p t e", e=E)
        first = sb("first", [P, TILES], f32)
        onehot = sb("onehot", [P, TILES, E], bf16)
        in_tile = slab[4].rearrange("p (e t) -> p e t", e=E)
        ones_et = sb("ones_et", [P, E * TILES], f32)
        upto = sb("upto", [P, E * TILES], f32)
        ahead = slab[5].rearrange("p (e t) -> p e t", e=E)
        total = sb("total", [P, E], f32)
        thresholds = sb("thresholds", [P, E, TILES], f32)
        over = slab[6].rearrange("p (e t) -> p e t", e=E)
        ntiles = sb("ntiles", [P, E], f32)
        tend = sb("tend", [P, E], f32)
        tstart = sb("tstart", [P, E], f32)
        shift = sb("shift", [P, E], f32)
        place = slab[7].rearrange("p (e t) -> p e t", e=E)
        place2 = slab[2].rearrange("p (t e) -> p t e", e=E)
        place3 = slab[3].rearrange("p (t e) -> p t e", e=E)
        slot_f = sb("slot_f", [P, TILES], f32)
        slot_of = sb("slot_of", [P, TILES], i32)
        tile_no = sb("tile_no", [1, SLOT_TILES, E - 1], f32)
        past = sb("past", [1, SLOT_TILES, E - 1], f32)
        expert_f = sb("expert_f", [1, SLOT_TILES], f32)
        expert = sb("expert", [1, SLOT_TILES], i32)

        xa = [sb(f"xa{k}", [P, C], f32) for k in range(2)]
        xr = [sb(f"xr{k}", [P, C], f32) for k in range(2)]
        token = [sb(f"token{k}", [P, 2], f32) for k in range(2)]
        sT = [[sb(f"sT{k}_{s}", [P, CC, P], f16) for s in ("hi", "lo")] for k in range(2)]
        free = rows[:, :, :].rearrange("p t c -> p (t c)")
        g = [free[:, k * I:(k + 1) * I].rearrange("p (i t) -> p i t", i=IC) for k in range(2)]
        h = [[free[:, 2 * I + n * (I // 2):2 * I + (n + 1) * (I // 2)].bitcast(f16)
              .rearrange("p (i t) -> p i t", i=IC) for n in (2 * k, 2 * k + 1)] for k in range(2)]
        room = [qbd[k][:, :, :, :, :, :].rearrange("p s c b h q -> p (s c b h q)").bitcast(f32) for k in range(2)]
        xbo, xbe, fin = ([room[k][:, n * C:(n + 1) * C] for k in range(2)] for n in range(3))
        y2, ng, z = (room[n % 2][:, (3 + n // 2) * C:(4 + n // 2) * C] for n in range(3))
        stats_a = sb("stats_a", [P, 6], f32)
        stats_b = sb("stats_b", [P, 6], f32)
        mv_a = sb("mv_a", [P, 2], f32)
        mv_b = sb("mv_b", [P, 2], f32)
        ve_a = sb("ve_a", [P, 1], f32)
        ve_b = sb("ve_b", [P, 1], f32)
        rs_a = sb("rs_a", [P, 1], f32)
        rs_b = sb("rs_b", [P, 1], f32)

        ps = ctx.enter_context(nc.psum_tensor("ps", [P, 8, 512], f32))
        ps_x = ps[:, 0, 0:CC * P].rearrange("p (k t) -> p k t", k=CC)
        ps_qk = ps[:, 0, :].rearrange("p (m t) -> p m t", m=2 * CC)
        ps_m = ps[:, 1, :]
        ps_aT = ps_m[:, 0:C].rearrange("p (b e q) -> p e b q", b=2, e=2)
        ps_s = [ps[:, 2 + k, :] for k in range(2)]
        ps_t = [ps[:, 4 + k, :] for k in range(2)]
        ps_o = ps[:, 6:6 + CC, 0:2 * PAIRS * 2 * (HD + 1)].rearrange("p c (n o) -> p c n o", o=2 * (HD + 1))
        ps_h = [ps[:, 2 * k:2 * k + 2, :] for k in range(2)]
        ps_y = [ps[:, 4 + k, 0:C] for k in range(2)]
        ps_sx = [ps[:, 6 + k, 0:CC * P].rearrange("p (k t) -> p k t", k=CC) for k in range(2)]

        attn_w_ld, ffn_w_ld = sem("attn_w_ld"), sem("ffn_w_ld")
        xin_ld = [sem(f"xin_ld{k}") for k in range(2)]
        xres_ld = [sem(f"xres_ld{k}") for k in range(2)]
        w1_ld, fill_st, disp_st = sem("w1_ld"), sem("fill_st"), sem("disp_st")
        consts_done, consts_step = sem("consts_done"), sem("consts_step")
        qbd_done = sem("qbd_done")
        whi_done, wlo_done = sem("whi_done"), sem("wlo_done")
        setupT_done, setupT_out = sem("setupT_done"), sem("setupT_out")
        xT_done, xh_done, xl_done = sem("xT_done"), sem("xh_done"), sem("xl_done")
        qk_done, qkh_done, qkl_done = sem("qk_done"), sem("qkh_done"), sem("qkl_done")
        kcar_done = sem("kcar_done")
        v_done, v_out, vlow_done, vhigh_done = sem("v_done"), sem("v_out"), sem("vlow_done"), sem("vhigh_done")
        s_done, mx_done, diag_done, st_done = sem("s_done"), sem("mx_done"), sem("diag_done"), sem("st_done")
        exp_done, pv_done = sem("exp_done"), sem("pv_done")
        rden_done, att_done, attT_done = sem("rden_done"), sem("att_done"), sem("attT_done")
        ah_done, al_done = sem("ah_done"), sem("al_done")
        proj_done, xrb_done, y_done = sem("proj_done"), sem("xrb_done"), sem("y_done")
        bn_done, mv_done, rstd_done = sem("bn_done"), sem("mv_done"), sem("rstd_done")
        x1_done, row_done, x1T_done, x1T_out = sem("x1_done"), sem("row_done"), sem("x1T_done"), sem("x1T_out")
        lg_done, lg_out = sem("lg_done"), sem("lg_out")
        w1h_done, w1l_done = sem("w1h_done"), sem("w1l_done")
        route_step, onehot_done, rank_done = sem("route_step"), sem("onehot_done"), sem("rank_done")
        slots_known = sem("slots_known")
        xa_ld = [sem(f"xa_ld{k}") for k in range(2)]
        xr_ld = [sem(f"xr_ld{k}") for k in range(2)]
        token_ld = [sem(f"token_ld{k}") for k in range(2)]
        sT_done, sh_done, sl_done = sem("sT_done"), sem("sh_done"), sem("sl_done")
        h_done, g_done, hh_done, hl_done = sem("h_done"), sem("g_done"), sem("hh_done"), sem("hl_done")
        ffn_done, y2_done, bna_done, mva_done = sem("ffn_done"), sem("y2_done"), sem("bna_done"), sem("mva_done")
        rsa_done, ng_done, z_done = sem("rsa_done"), sem("ng_done"), sem("z_done")
        bnb_done, mvb_done, rsb_done, fin_done = sem("bnb_done"), sem("mvb_done"), sem("rsb_done"), sem("fin_done")
        veps_done, vea_done, veb_done = sem("veps_done"), sem("vea_done"), sem("veb_done")
        xbo_done, xbe_done = sem("xbo_done"), sem("xbe_done")
        out_st = [sem(f"out_st{k}") for k in range(2)]

        ATTN_LOADS, FFN_LOADS = 6, 6
        N_CONSTS = 1

        def apart(eng):
            eng.wait_ge(attn_w_ld, 16 * ATTN_LOADS)

        def variant(t):
            if isinstance(t, int):
                return min(t % SEQ, 1)
            return (t % SEQ + (SEQ - 1)) // SEQ

        def walk_tokens(eng, body):
            body(-1, 1, -1, True, False, False)
            body(0, 0, 0, True, True, False)
            body(1, 1, 0, True, True, True)
            body(2, 0, 1, True, True, True)
            with eng.Fori(0, (TILES - 4) // 2) as i:
                body(2 * i + 3, 1, i + 1, True, True, True)
                body(2 * i + 4, 0, i + 2, True, True, True)
            body(TILES - 1, 1, (TILES - 1) // 2, False, True, True)
            body(TILES, 0, TILES // 2, False, False, True)

        def walk_slots(eng, body):
            body(-2, 0, -1, True, False, False, False)
            body(-1, 1, -1, True, True, False, False)
            body(0, 0, 0, True, True, True, False)
            body(1, 1, 0, True, True, True, True)
            body(2, 0, 1, True, True, True, True)
            with eng.Fori(0, (SLOT_TILES - 5) // 2) as i:
                body(2 * i + 3, 1, i + 1, True, True, True, True)
                body(2 * i + 4, 0, i + 2, True, True, True, True)
            last = SLOT_TILES - 1
            body(last - 1, 1, (last - 1) // 2, False, True, True, True)
            body(last, 0, last // 2, False, False, True, True)
            body(last + 1, 1, (last + 1) // 2, False, False, False, True)

        block = ctx.enter_context(nc.Block())

        @block.sync
        def _(sp):
            sp.dma_start(xin[0][:, :], x_rows[0]).then_inc(xin_ld[0], 16)
            sp.dma_start(wa_in[:, :, :], w_attn.rearrange("(k p) n -> p k n", p=P)).then_inc(attn_w_ld, 16)
            sp.dma_start(xin[1][:, :], x_rows[1]).then_inc(xin_ld[1], 16)
            sp.dma_start(bqk_in[:, :], b_attn[0:2 * C].unsqueeze(0)).then_inc(attn_w_ld, 16)
            sp.dma_start(bv[:, :], b_attn[2 * C:3 * C].unsqueeze(0).broadcast_to([P, C])).then_inc(attn_w_ld, 16)
            for o in range(2):
                sp.dma_start(wp_in[:, o, :], w_proj.rearrange("(n o d) c -> o n d c", o=2, d=HD)[o])\
                    .then_inc(attn_w_ld, 16)
            sp.dma_start(bp[:, :], b_proj.unsqueeze(0).broadcast_to([P, C])).then_inc(attn_w_ld, 16)

            sp.wait_ge(consts_done, N_CONSTS)
            sp.dma_start(slot_tiles.rearrange("j p c -> p j c"),
                         fill[:, :].unsqueeze(1).broadcast_to([P, SLOT_TILES, ROW])).then_inc(fill_st, 16)

            def body(t, p, hf):
                if not isinstance(t, int) or t + 2 < TILES:
                    wait(sp, xT_done, t + 1)
                    sp.dma_start(xin[p][:, :], x_rows[t + 2]).then_inc(xin_ld[p], 16)
                wait(sp, y_done, t - 1)
                sp.dma_start(xres[p][:, :], x_rows[t]).then_inc(xres_ld[p], 16)
                if p == 0:
                    wait(sp, w1l_done, 2 * hf)
                    sp.dma_start(w1_in[:, :], w1_units[hf]).then_inc(w1_ld, 16)

            for t in range(3):
                body(t, t % 2, t // 2)
            with sp.Fori(0, (TILES - 6) // 2) as i:
                body(2 * i + 3, 1, i + 1)
                body(2 * i + 4, 0, i + 2)
            for t in range(TILES - 3, TILES):
                body(t, t % 2, t // 2)

            sp.wait_ge(fill_st, 16)
            sp.wait_ge(disp_st, 16 * TILES)
            sp.dma_start(xa[0][:, :], slot_tiles[0][:, 0:C]).then_inc(xa_ld[0], 16)
            sp.dma_start(xa[1][:, :], slot_tiles[1][:, 0:C]).then_inc(xa_ld[1], 16)
            sp.dma_start(xr[0][:, :], slot_tiles[0][:, 0:C]).then_inc(xr_ld[0], 16)
            sp.wait_ge(sT_done, 1)
            sp.dma_start(xa[0][:, :], slot_tiles[2][:, 0:C]).then_inc(xa_ld[0], 16)

            def loads(j, p, hf):
                if not isinstance(j, int) or j + 3 < SLOT_TILES:
                    sp.wait_ge(sT_done, j + 2)
                    sp.dma_start(xa[1 - p][:, :], slot_tiles[j + 3][:, 0:C]).then_inc(xa_ld[1 - p], 16)
                if not isinstance(j, int) or j + 1 < SLOT_TILES:
                    wait(sp, xbe_done, j)
                    sp.dma_start(xr[1 - p][:, :], slot_tiles[j + 1][:, 0:C]).then_inc(xr_ld[1 - p], 16)
                wait(sp, out_st[p], 16 * hf)
                sp.dma_start(token[p][:, :], slot_tiles[j][:, C - 1:ROW]).then_inc(token_ld[p], 16)

            for j in range(3):
                loads(j, j % 2, j // 2)
            with sp.Fori(0, (SLOT_TILES - 7) // 2) as i:
                loads(2 * i + 3, 1, i + 1)
                loads(2 * i + 4, 0, i + 2)
            for j in range(SLOT_TILES - 4, SLOT_TILES):
                loads(j, j % 2, j // 2)
            sp.wait_ge(out_st[0], 16 * ((SLOT_TILES + 1) // 2))
            sp.wait_ge(out_st[1], 16 * (SLOT_TILES // 2))

        @block.gpsimd
        def _(pool):
            step = [0]

            def link(ins):
                step[0] += 1
                ins.then_inc(consts_step, 1)
                pool.wait_ge(consts_step, step[0])

            link(nc.gpsimd.memset(ident[:, :], 0.0))
            link(nc.gpsimd.affine_select(out=ident[:, :], in_=ident[:, :], compare_op=ALU.not_equal, fill=1.0,
                                         base=0, pattern=[[-1, P]], channel_multiplier=1))
            link(nc.gpsimd.tensor_copy(ident_b[:, :], ident[:, :]))
            link(nc.gpsimd.memset(fill[:, :], 0.0))
            link(nc.gpsimd.memset(fill[:, C:ROW].bitcast(i32), NO_TOKEN))
            link(nc.gpsimd.memset(band[:, :], 1.0))
            link(nc.gpsimd.affine_select(out=band[:, :], in_=band[:, :], compare_op=ALU.is_ge, fill=0.0,
                                         base=0, pattern=[[-HD, CH]], channel_multiplier=1))
            link(nc.gpsimd.affine_select(out=band[:, :], in_=band[:, :], compare_op=ALU.is_ge, fill=0.0,
                                         base=HD - 1, pattern=[[HD, CH]], channel_multiplier=-1))
            nc.gpsimd.memset(bqk[:, :], 0.0)
            nc.gpsimd.memset(ones16[:, :], 1.0)
            link(nc.gpsimd.memset(mask_q[:, :, :], 0.0))
            for e in range(2):
                r = slice(BLK * e, BLK * e + BLK)
                for sign, base in ((1, 0), (-1, BLK)):
                    link(nc.gpsimd.affine_select(
                        out=mask_q[r, :, :], in_=mask_q[r, :, :], compare_op=ALU.is_ge, fill=MASKED,
                        base=base, pattern=[[0, 2], [sign, P]], channel_multiplier=-sign))
            link(nc.gpsimd.memset(mask_q[:, 0, 0:BLK], MASKED))
            nc.gpsimd.memset(minus1[:, :], -1.0)
            for k in range(2):
                nc.gpsimd.memset(v_cur[k][:, :, :], 1.0)
                nc.gpsimd.memset(v_mid[k][:, :, :], 1.0)
            nc.gpsimd.memset(k_[0][:, :, :, 0:BLK], 0.0)
            link(nc.gpsimd.memset(ones_b[:, :], 1.0))
            link(nc.gpsimd.affine_select(out=before[:, :], in_=ones_b[:, :], compare_op=ALU.is_ge, fill=0.0,
                                         base=-1, pattern=[[1, P]], channel_multiplier=-1))
            nc.gpsimd.iota(rows[:, :, C:ROW].bitcast(i32), pattern=[[P, TILES], [0, 1]], base=0,
                           channel_multiplier=1)
            nc.gpsimd.iota(desc[:, :], pattern=[[-1, E]], base=E, channel_multiplier=0,
                           allow_small_or_imprecise_dtypes=True)
            nc.gpsimd.memset(ones_et[:, :], 1.0)
            for const, value in ((power, -0.5), (zero, 0.0), (eps_outer, EPS_OUTER), (eps_ffn, EPS_FFN)):
                nc.gpsimd.memset(const[:, :], value)
            nc.gpsimd.iota(thresholds[:, :, :], pattern=[[0, E], [P, TILES]], base=0, channel_multiplier=0,
                           allow_small_or_imprecise_dtypes=True)
            nc.gpsimd.iota(tile_no[:, :, :], pattern=[[1, SLOT_TILES], [0, E - 1]], base=0,
                           channel_multiplier=0, allow_small_or_imprecise_dtypes=True).then_inc(consts_done, 1)

            pool.wait_ge(attn_w_ld, 16 * ATTN_LOADS)

            def body(t, p, hf, nxt, cur, prv):
                if cur:
                    pool.wait_ge(qkl_done, t + 1)
                    wait(pool, st_done, 4 * t)
                    nc.gpsimd.tensor_tensor(k_[1 - p][:, :, :, 0:BLK], k_[p][:, :, :, P:P + BLK],
                                            zero[:, :].unsqueeze(2).unsqueeze(3).broadcast_to([P, 2, CC, BLK]),
                                            ALU.add)\
                        .then_inc(kcar_done, 1)

                def diagonals(u):
                    pool.wait_ge(mx_done, 4 * t + u + 1)
                    wait(pool, st_done, 4 * t + u - 1)
                    nc.gpsimd.tensor_tensor(
                        diag[u % 2][:, :, :], ident_b[:, :].unsqueeze(1).broadcast_to([P, PAIRS, P]),
                        mx[u % 2][:, :].unsqueeze(2).broadcast_to([P, PAIRS, P]), ALU.mult).then_inc(diag_done, 1)

                if cur:
                    diagonals(0)
                if prv:
                    pool.wait_ge(xres_ld[1 - p], 16 * (hf + p))
                    nc.gpsimd.tensor_tensor(xres[1 - p][:, :], xres[1 - p][:, :], bp[:, :], ALU.add)\
                        .then_inc(xrb_done, 1)
                if cur:
                    diagonals(1)
                    diagonals(2)
                if prv:
                    pool.wait_ge(mv_done, t)
                    wait(pool, x1_done, t - 1)
                    nc.gpsimd.tensor_tensor(veps[:, :], meanvar[:, 1:2], eps_outer[:, :], ALU.add)\
                        .then_inc(veps_done, 1)
                    pool.wait_ge(veps_done, t)
                    nc.gpsimd.tensor_tensor(rstd[:, :], veps[:, :], power[:, :], ALU.pow).then_inc(rstd_done, 1)
                if cur:
                    diagonals(3)
                if prv:
                    apart(pool)
                    pool.wait_ge(x1_done, t)
                    nc.gpsimd.tensor_copy(rows[:, t - 1, 0:C], x1[:, :]).then_inc(row_done, 1)

            walk_tokens(pool, body)

            pool.wait_ge(row_done, TILES)
            pool.wait_ge(fill_st, 16)
            pool.wait_ge(slots_known, 1)
            for t in range(TILES):
                nc.gpsimd.indirect_dma_start(
                    out=slots, out_offset=bass.IndirectOffsetOnAxis(ap=slot_of[:, t:t + 1], axis=0),
                    in_=rows[:, t, :], in_offset=None, bounds_check=SLOTS - 1, oob_is_err=False)\
                    .then_inc(disp_st, 16)
            pool.wait_ge(ffn_w_ld, 16 * FFN_LOADS)

            def body3(j, p, hf, load, up, down, norm):
                if norm:
                    pool.wait_ge(mva_done, j)
                    wait(pool, z_done, j - 1)
                    nc.gpsimd.tensor_tensor(ve_a[:, :], mv_a[:, 1:2], eps_ffn[:, :], ALU.add)\
                        .then_inc(vea_done, 1)
                    pool.wait_ge(vea_done, j)
                    nc.gpsimd.tensor_tensor(rs_a[:, :], ve_a[:, :], power[:, :], ALU.pow)\
                        .then_inc(rsa_done, 1)
                if down:
                    pool.wait_ge(xr_ld[p], 16 * (hf + 1))
                    wait(pool, y2_done, j - 1)
                    nc.gpsimd.tensor_tensor(xbo[p], xr[p][:, :], bo[:, :], ALU.add).then_inc(xbo_done, 1)
                    wait(pool, z_done, j - 1)
                    nc.gpsimd.tensor_tensor(xbe[p], xr[p][:, :], bet[:, :], ALU.add).then_inc(xbe_done, 1)
                if norm:
                    pool.wait_ge(mvb_done, j)
                    wait(pool, fin_done, j - 1)
                    nc.gpsimd.tensor_tensor(ve_b[:, :], mv_b[:, 1:2], eps_outer[:, :], ALU.add)\
                        .then_inc(veb_done, 1)
                    pool.wait_ge(veb_done, j)
                    nc.gpsimd.tensor_tensor(rs_b[:, :], ve_b[:, :], power[:, :], ALU.pow)\
                        .then_inc(rsb_done, 1)
                if norm:
                    apart(pool)
                    pool.wait_ge(fin_done, j)
                    pool.wait_ge(token_ld[1 - p], 16 * (hf + p))
                    nc.gpsimd.indirect_dma_start(
                        out=out_rows,
                        out_offset=bass.IndirectOffsetOnAxis(ap=token[1 - p][:, 1:2].bitcast(i32), axis=0),
                        in_=fin[1 - p], in_offset=None, bounds_check=N - 1, oob_is_err=False)\
                        .then_inc(out_st[1 - p], 16)

            walk_slots(pool, body3)

        @block.scalar
        def _(act):
            for dst, src in ((wr_in[:, :], w_router), (b1_in[:, :], b1.rearrange("e (k p) -> (e k) p", p=P)),
                             (wo_in[:, :, :], w_out.rearrange("(k p) n -> p k n", p=P)),
                             (bo[:, :], b_out.unsqueeze(0).broadcast_to([P, C])),
                             (gam[:, :], gamma.unsqueeze(0).broadcast_to([P, C])),
                             (bet[:, :], beta.unsqueeze(0).broadcast_to([P, C]))):
                act.dma_start(dst, src).then_inc(ffn_w_ld, 16)
            act.wait_ge(attn_w_ld, 16 * ATTN_LOADS)
            act.wait_ge(consts_done, N_CONSTS)
            nc.scalar.activation(wa[0][:, :, :], wa_in[:, :, :], ACT.Copy, scale=W_UP).then_inc(whi_done, 1)
            nc.scalar.activation(bqk[0:1, :], bqk_in[:, :], ACT.Copy, scale=W_UP).then_inc(whi_done, 1)
            nc.scalar.activation(wp[0][:, :, :], wp_in[:, :, :], ACT.Copy, scale=W_UP).then_inc(whi_done, 1)
            act.wait_ge(ffn_w_ld, 16 * FFN_LOADS)
            nc.scalar.activation(wo[0][:, :, :], wo_in[:, :, :], ACT.Copy, scale=W_UP).then_inc(whi_done, 1)
            act.wait_ge(setupT_done, 1)
            nc.scalar.activation(wrT[:, :, :], ps[:, 1, 0:CC * E].rearrange("p (k e) -> p k e", k=CC), ACT.Copy)
            nc.scalar.activation(b1T[:, :], ps[:, 1, P:P + E * IC], ACT.Copy).then_inc(setupT_out, 1)

            def body(t, p, hf, nxt, cur, prv):
                if nxt:
                    act.wait_ge(xT_done, t + 2)
                    wait(act, v_done, t + 1)
                    nc.scalar.activation(xT[0][:, :, :], ps_x, ACT.Copy).then_inc(xh_done, 1)
                if prv:
                    act.wait_ge(attT_done, t)
                    wait(act, proj_done, t - 1)
                    nc.scalar.activation(attT[0][:, :, :, :], ps_aT, ACT.Copy).then_inc(ah_done, 1)
                    piece, cols = hf + p - 1, slice((1 - p) * I // 2, (2 - p) * I // 2)
                    act.wait_ge(w1_ld, 16 * (hf + p))
                    nc.scalar.activation(w1s[0][:, piece, cols], w1_in[:, cols], ACT.Copy, scale=W_UP)\
                        .then_inc(w1h_done, 1)
                if nxt:
                    act.wait_ge(qk_done, t + 2)
                    wait(act, st_done, 4 * t)
                    wait(act, kcar_done, t)
                    wait(act, qbd_done, t + 1)
                    nc.scalar.activation(k_[1 - p][:, 0, :, BLK:BLK + P], ps_qk[:, CC:2 * CC, :], ACT.Copy,
                                         scale=W_DOWN)
                    nc.scalar.activation(q[:, 0, :, :, :].rearrange("p c b q -> p c (b q)"), ps_qk[:, 0:CC, :],
                                         ACT.Copy, scale=W_DOWN).then_inc(qkh_done, 1)

                def exps(u):
                    act.wait_ge(st_done, 4 * t + u + 1)
                    wait(act, pv_done, 4 * t + u - 3)
                    nc.scalar.activation(probs[u][:, :, :], ps_t[u % 2].rearrange("p (a q) -> p a q", a=PAIRS),
                                         ACT.Exp, scale=SCALE).then_inc(exp_done, 1)

                if cur:
                    exps(0)
                    act.wait_ge(v_out, t + 1)
                    wait(act, pv_done, 4 * t)
                    nc.scalar.activation(v_mid[1 - p][0:BLK, :, 0:HD], v_cur[p][BLK:P, :, 0:HD], ACT.Copy)\
                        .then_inc(vlow_done, 1)
                    exps(1)
                    exps(2)
                    exps(3)
                if nxt:
                    act.wait_ge(v_out, t + 2)
                    nc.scalar.activation(v_mid[1 - p][BLK:P, :, 0:HD], v_cur[1 - p][0:BLK, :, 0:HD], ACT.Copy)\
                        .then_inc(vhigh_done, 1)
                if prv:
                    act.wait_ge(x1T_done, t)
                    wait(act, lg_done, t - 1)
                    nc.scalar.activation(x1T[:, :, :], ps_x, ACT.Copy).then_inc(x1T_out, 1)
                    act.wait_ge(lg_done, t)
                    nc.scalar.activation(logits[:, t - 1, :], ps_m[:, 0:E], ACT.Copy).then_inc(lg_out, 1)

            walk_tokens(act, body)

            def body3(j, p, hf, load, up, down, norm):
                if load:
                    act.wait_ge(sT_done, j + 3)
                    wait(act, h_done, 2 * j + 2)
                    nc.scalar.activation(sT[p][0][:, :, :], ps_sx[p], ACT.Copy).then_inc(sh_done, 1)
                if up:
                    e = act.value_load(expert[0:1, bass.ds(j + 1, 1)], min_val=0, max_val=E - 1)
                    wait(act, hl_done, 2 * j)
                    for half in range(2):
                        act.wait_ge(h_done, 2 * j + 3 + half)
                        ics = range(half * IC // 2, (half + 1) * IC // 2)
                        for ic in ics:
                            col = (ic % (IC // 2)) * P
                            last = nc.scalar.activation(
                                g[1 - p][:, ic, :], ps_h[1 - p][:, half, col:col + P], ACT.Gelu,
                                bias=b1T[:, bass.ds(e * IC + ic, 1)], scale=W_DOWN)
                        last.then_inc(g_done, 1)
                        act.wait_ge(g_done, 2 * j + 3 + half)
                        wait(act, ffn_done, j)
                        nc.scalar.activation(h[1 - p][0][:, ics[0]:ics[-1] + 1, :],
                                             g[1 - p][:, ics[0]:ics[-1] + 1, :], ACT.Copy).then_inc(hh_done, 1)

            act.wait_ge(slots_known, 1)
            walk_slots(act, body3)

        @block.vector
        def _(dve):
            dve.wait_ge(consts_done, N_CONSTS)
            dve.wait_ge(whi_done, 1)
            nc.vector.scalar_tensor_tensor(wa[1][:, :, :], wa_in[:, :, :], W_UP, wa[0][:, :, :],
                                           ALU.mult, ALU.subtract).then_inc(wlo_done, 1)
            dve.wait_ge(whi_done, 2)
            nc.vector.scalar_tensor_tensor(bqk[32:33, :], bqk_in[:, :], W_UP, bqk[0:1, :],
                                           ALU.mult, ALU.subtract).then_inc(wlo_done, 1)
            dve.wait_ge(whi_done, 3)
            nc.vector.scalar_tensor_tensor(wp[1][:, :, :], wp_in[:, :, :], W_UP, wp[0][:, :, :],
                                           ALU.mult, ALU.subtract).then_inc(wlo_done, 1)
            dve.wait_ge(whi_done, 4)
            nc.vector.scalar_tensor_tensor(wo[1][:, :, :], wo_in[:, :, :], W_UP, wo[0][:, :, :],
                                           ALU.mult, ALU.subtract).then_inc(wlo_done, 1)

            def body(t, p, hf, nxt, cur, prv):
                def maxima(u):
                    dve.wait_ge(s_done, 4 * t + u + 1)
                    wait(dve, diag_done, 4 * t + u - 1)
                    nc.vector.tensor_reduce(mx[u % 2][:, :], ps_s[u % 2].rearrange("p (a k) -> p a k", k=P),
                                            AX.X, ALU.max).then_inc(mx_done, 1)

                def spread(s):
                    for n in range(CH):
                        last = nc.vector.tensor_scalar(
                            qbd[1 - p][:, s, :, :, n, :].rearrange("p c b q -> p (c b) q"),
                            q[:, s, :, :, :].rearrange("p c b q -> p (c b) q"), band[:, n:n + 1], None, ALU.mult)
                    return last

                if prv:
                    dve.wait_ge(pv_done, 4 * t)
                    wait(dve, att_done, t - 1)
                    for e in range(2):
                        r, one = slice(BLK * e, BLK * e + BLK), e * (HD + 1) + HD
                        last = nc.vector.reciprocal(rden[r, :, :], ps_o[r, :, :, one])
                    last.then_inc(rden_done, 1)
                    dve.wait_ge(rden_done, t)
                    wait(dve, attT_done, t - 1)
                    for e in range(2):
                        r, own = slice(BLK * e, BLK * e + BLK), e * (HD + 1)
                        for c in range(CC):
                            last = nc.vector.tensor_tensor(
                                att[r, :, c, :, :].rearrange("p b a d -> p b a d"),
                                ps_o[r, c, :, own:own + HD].rearrange("p (b a) d -> p b a d", b=2),
                                rden[r, c, :].rearrange("p (b a) -> p b a", b=2).unsqueeze(3)
                                .broadcast_to([BLK, 2, PAIRS, HD]), ALU.mult)
                    last.then_inc(att_done, 1)
                if cur:
                    maxima(0)
                if nxt:
                    dve.wait_ge(xh_done, t + 2)
                    wait(dve, v_done, t + 1)
                    nc.vector.tensor_tensor(xT[1][:, :, :], ps_x, xT[0][:, :, :], ALU.subtract)\
                        .then_inc(xl_done, 1)
                if cur:
                    maxima(1)
                if prv:
                    dve.wait_ge(ah_done, t)
                    wait(dve, proj_done, t - 1)
                    nc.vector.tensor_tensor(attT[1][:, :, :, :], ps_aT, attT[0][:, :, :, :], ALU.subtract)\
                        .then_inc(al_done, 1)
                    piece, cols = hf + p - 1, slice((1 - p) * I // 2, (2 - p) * I // 2)
                    dve.wait_ge(w1h_done, t)
                    nc.vector.scalar_tensor_tensor(w1s[1][:, piece, cols], w1_in[:, cols], W_UP,
                                                   w1s[0][:, piece, cols], ALU.mult, ALU.subtract)\
                        .then_inc(w1l_done, 1)
                if nxt:
                    dve.wait_ge(qkh_done, t + 2)
                    wait(dve, st_done, 4 * t)
                    wait(dve, kcar_done, t)
                    wait(dve, qbd_done, t + 1)
                    nc.vector.scalar_tensor_tensor(k_[1 - p][:, 1, :, BLK:BLK + P], ps_qk[:, CC:2 * CC, :], W_DOWN,
                                                   k_[1 - p][:, 0, :, BLK:BLK + P], ALU.mult, ALU.subtract)
                    nc.vector.scalar_tensor_tensor(
                        q[:, 1, :, :, :].rearrange("p c b q -> p c (b q)"), ps_qk[:, 0:CC, :], W_DOWN,
                        q[:, 0, :, :, :].rearrange("p c b q -> p c (b q)"), ALU.mult, ALU.subtract)\
                        .then_inc(qkl_done, 1)
                if prv:
                    dve.wait_ge(proj_done, t)
                    dve.wait_ge(xrb_done, t)
                    wait(dve, x1_done, t - 1)
                    nc.vector.scalar_tensor_tensor(y[:, :], ps_m[:, 0:C], W_DOWN, xres[1 - p][:, :],
                                                   ALU.mult, ALU.add).then_inc(y_done, 1)
                if cur:
                    maxima(2)
                if prv:
                    dve.wait_ge(y_done, t)
                    nc.vector.bn_stats(stats[:, :], y[:, :]).then_inc(bn_done, 1)
                    apart(dve)
                    dve.wait_ge(bn_done, t)
                    wait(dve, rstd_done, t - 1)
                    nc.vector.bn_aggr(meanvar[:, :], stats[:, :]).then_inc(mv_done, 1)
                if cur:
                    maxima(3)
                if nxt:
                    spread(0)
                if prv:
                    dve.wait_ge(rstd_done, t)
                    wait(dve, x1T_done, t - 1)
                    wait(dve, row_done, t - 1)
                    nc.vector.tensor_scalar(x1[:, :], y[:, :], meanvar[:, 0:1], rstd[:, :],
                                            ALU.subtract, ALU.mult).then_inc(x1_done, 1)
                if nxt:
                    dve.wait_ge(qkl_done, t + 2)
                    spread(1).then_inc(qbd_done, 1)
                    dve.wait_ge(v_done, t + 2)
                    wait(dve, pv_done, 4 * t)
                    wait(dve, vlow_done, t)
                    wait(dve, vhigh_done, t)
                    nc.vector.scalar_tensor_tensor(
                        v_cur[1 - p][:, :, 0:HD], ps_m[:, 0:C].rearrange("p (h d) -> p h d", h=HEADS), W_DOWN,
                        bv[:, :].rearrange("p (h d) -> p h d", h=HEADS), ALU.mult, ALU.add).then_inc(v_out, 1)

            walk_tokens(dve, body)

            step = [0]

            def link(ins):
                step[0] += 1
                ins.then_inc(route_step, 1)
                dve.wait_ge(route_step, step[0])

            lg = logits[:, :, :]
            over_e = lambda a: a.unsqueeze(2).broadcast_to([P, TILES, E])
            per_e = desc[:, :].unsqueeze(1).broadcast_to([P, TILES, E])
            dve.wait_ge(lg_out, TILES)
            link(nc.vector.tensor_reduce(top[:, :], lg, AX.X, ALU.max))
            link(nc.vector.tensor_tensor(hit[:, :, :], lg, over_e(top[:, :]), ALU.is_equal))
            link(nc.vector.tensor_tensor(pick[:, :, :], hit[:, :, :], per_e, ALU.mult))
            link(nc.vector.tensor_reduce(first[:, :], pick[:, :, :], AX.X, ALU.max))
            nc.vector.tensor_tensor(onehot[:, :, :], per_e, over_e(first[:, :]), ALU.is_equal)\
                .then_inc(onehot_done, 1)
            dve.wait_ge(rank_done, 1)
            tot_ps = ps[:, 1, 0:TILES * E].rearrange("p (t e) -> p e t", e=E)
            link(nc.vector.tensor_copy(in_tile[:, :, :], tot_ps))
            link(nc.vector.tensor_tensor_scan(upto[:, :], ones_et[:, :], in_tile[:, :, :].rearrange("p e t -> p (e t)"),
                                              0.0, ALU.mult, ALU.add))
            link(nc.vector.tensor_tensor(ahead[:, :, :], upto[:, :].rearrange("p (e t) -> p e t", e=E),
                                         in_tile[:, :, :], ALU.subtract))
            link(nc.vector.tensor_reduce(total[:, :], in_tile[:, :, :], AX.X, ALU.add))
            link(nc.vector.tensor_tensor(over[:, :, :], total[:, :].unsqueeze(2).broadcast_to([P, E, TILES]),
                                         thresholds[:, :, :], ALU.is_gt))
            link(nc.vector.tensor_reduce(ntiles[:, :], over[:, :, :], AX.X, ALU.add))
            link(nc.vector.tensor_tensor_scan(tend[:, :], ones_et[:, 0:E], ntiles[:, :], 0.0, ALU.mult, ALU.add))
            link(nc.vector.tensor_tensor(tstart[:, :], tend[:, :], ntiles[:, :], ALU.subtract))
            link(nc.vector.scalar_tensor_tensor(shift[:, :], tstart[:, :], float(P), ahead[:, :, 0],
                                                ALU.mult, ALU.subtract))
            link(nc.vector.tensor_tensor(place[:, :, :], ahead[:, :, :],
                                         shift[:, :].unsqueeze(2).broadcast_to([P, E, TILES]), ALU.add))
            link(nc.vector.tensor_tensor(place2[:, :, :], ps[:, 0, 0:TILES * E].rearrange("p (t e) -> p t e", e=E),
                                         place[:, :, :].rearrange("p e t -> p t e"), ALU.add))
            link(nc.vector.tensor_tensor(place3[:, :, :], place2[:, :, :], onehot[:, :, :], ALU.mult))
            link(nc.vector.tensor_reduce(slot_f[:, :], place3[:, :, :], AX.X, ALU.add))
            link(nc.vector.tensor_copy(slot_of[:, :], slot_f[:, :]))
            link(nc.vector.tensor_tensor(past[:, :, :], tile_no[:, :, :],
                                         tend[0:1, 0:E - 1].unsqueeze(1).broadcast_to([1, SLOT_TILES, E - 1]),
                                         ALU.is_ge))
            link(nc.vector.tensor_reduce(expert_f[:, :], past[:, :, :], AX.X, ALU.add))
            nc.vector.tensor_copy(expert[:, :], expert_f[:, :]).then_inc(slots_known, 1)

            def body3(j, p, hf, load, up, down, norm):
                def split(j, buf, half):
                    a, b = half * IC // 2, (half + 1) * IC // 2
                    dve.wait_ge(hh_done, 2 * j + 1 + half)
                    wait(dve, ffn_done, j - 1)
                    nc.vector.tensor_tensor(h[buf][1][:, a:b, :], g[buf][:, a:b, :], h[buf][0][:, a:b, :],
                                            ALU.subtract).then_inc(hl_done, 1)

                if norm:
                    dve.wait_ge(ffn_done, j)
                    dve.wait_ge(xbo_done, j)
                    wait(dve, ng_done, j - 1)
                    nc.vector.scalar_tensor_tensor(y2, ps_y[1 - p], W_DOWN, xbo[1 - p],
                                                   ALU.mult, ALU.add).then_inc(y2_done, 1)
                    dve.wait_ge(y2_done, j)
                    nc.vector.bn_stats(stats_a[:, :], y2).then_inc(bna_done, 1)
                    apart(dve)
                    dve.wait_ge(bna_done, j)
                    wait(dve, rsa_done, j - 1)
                    nc.vector.bn_aggr(mv_a[:, :], stats_a[:, :]).then_inc(mva_done, 1)
                if down:
                    split(j, p, 1)
                if load:
                    dve.wait_ge(sh_done, j + 3)
                    wait(dve, h_done, 2 * j + 2)
                    nc.vector.tensor_tensor(sT[p][1][:, :, :], ps_sx[p], sT[p][0][:, :, :], ALU.subtract)\
                        .then_inc(sl_done, 1)
                if norm:
                    dve.wait_ge(mva_done, j)
                    wait(dve, z_done, j - 1)
                    nc.vector.scalar_tensor_tensor(ng, y2, mv_a[:, 0:1], gam[:, :],
                                                   ALU.subtract, ALU.mult).then_inc(ng_done, 1)
                    dve.wait_ge(rsa_done, j)
                    dve.wait_ge(ng_done, j)
                    dve.wait_ge(xbe_done, j)
                    wait(dve, fin_done, j - 1)
                    nc.vector.scalar_tensor_tensor(z, ng, rs_a[:, :], xbe[1 - p],
                                                   ALU.mult, ALU.add).then_inc(z_done, 1)
                    dve.wait_ge(z_done, j)
                    nc.vector.bn_stats(stats_b[:, :], z).then_inc(bnb_done, 1)
                    apart(dve)
                    dve.wait_ge(bnb_done, j)
                    wait(dve, rsb_done, j - 1)
                    nc.vector.bn_aggr(mv_b[:, :], stats_b[:, :]).then_inc(mvb_done, 1)
                if up:
                    split(j + 1, 1 - p, 0)
                if norm:
                    dve.wait_ge(rsb_done, j)
                    wait(dve, out_st[1 - p], 16 * (hf + p - 1))
                    nc.vector.tensor_scalar(fin[1 - p], z, mv_b[:, 0:1], rs_b[:, :],
                                            ALU.subtract, ALU.mult).then_inc(fin_done, 1)

            walk_slots(dve, body3)

        @block.tensor
        def _(pe):
            mm = nc.tensor.matmul

            def product(dst, left, right, start=True, stop=True):
                terms = [(l, r) for k in range(len(left)) for l, r in
                         ((left[k][0], right[k][0]), (left[k][1], right[k][0]), (left[k][0], right[k][1]))]
                for n, (l, r) in enumerate(terms):
                    last = mm(dst, l, r, start=start and n == 0, stop=stop and n == len(terms) - 1)
                return last

            pe.wait_ge(consts_done, N_CONSTS)
            pe.wait_ge(ffn_w_ld, 16 * FFN_LOADS)
            for k in range(CC):
                nc.tensor.transpose(ps[:, 1, k * E:(k + 1) * E], wr_in[:, k * P:(k + 1) * P], ident[0:E, 0:E])
            nc.tensor.transpose(ps[:, 1, P:P + E * IC], b1_in[:, :], ident[0:E * IC, 0:E * IC])\
                .then_inc(setupT_done, 1)
            pe.wait_ge(setupT_out, 1)

            def body(t, p, hf, nxt, cur, prv):
                var = variant(t) if cur else 0

                def mask(b):
                    return mask_q[:, bass.ds(var, 1), :].rearrange("p a k -> p (a k)") if b == 0 else mask_q[:, 1, :]

                def scores(u):
                    c, b = u // 2, u % 2
                    if u == 0:
                        pe.wait_ge(qbd_done, t + 1)
                        wait(pe, kcar_done, t)
                    wait(pe, mx_done, 4 * t + u - 1)
                    mm(ps_s[u % 2].rearrange("p (a k) -> p a k", a=PAIRS), ident_b[:, :],
                       mask(b).unsqueeze(1).broadcast_to([P, PAIRS, P]),
                       start=True, stop=False, skip_group_check=True)
                    for a in range(PAIRS):
                        last = mm(ps_s[u % 2][:, a * P:(a + 1) * P],
                                  qbd[p][:, 0, c, b, 2 * a:2 * a + 2, :].rearrange("p e q -> p (e q)"),
                                  k_[p][:, 0, c, BLK * b:BLK * b + P],
                                  start=False, stop=a == PAIRS - 1, skip_group_check=True)
                    last.then_inc(s_done, 1)

                def scores_t(u):
                    c, b = u // 2, u % 2
                    wait(pe, exp_done, 4 * t + u - 1)
                    mm(ps_t[u % 2].rearrange("p (a q) -> p a q", a=PAIRS), mask(b),
                       ident_b[:, :].unsqueeze(1).broadcast_to([P, PAIRS, P]),
                       start=True, stop=False, skip_group_check=True)
                    for klo, qlo in ((0, 0), (1, 0), (0, 1)):
                        mm(ps_t[u % 2], k_[p][:, klo, c, BLK * b:BLK * b + P],
                           qbd[p][:, qlo, c, b, :, :].rearrange("p h q -> p (h q)"),
                           start=False, stop=False, skip_group_check=True)

                def less_maxima(u):
                    pe.wait_ge(diag_done, 4 * t + u + 1)
                    mm(ps_t[u % 2], minus1[:, :], diag[u % 2][:, :, :].rearrange("p a q -> p (a q)"),
                       start=False, stop=True, skip_group_check=True).then_inc(st_done, 1)

                def values(u):
                    c, b = u // 2, u % 2
                    pe.wait_ge(exp_done, 4 * t + u + 1)
                    if u == 0:
                        pe.wait_ge(vhigh_done, t + 1)
                        wait(pe, vlow_done, t)
                        wait(pe, att_done, t)
                    for a in range(PAIRS):
                        h0 = CH * c + 2 * a
                        last = mm(ps_o[:, c, b * PAIRS + a, :], probs[u][:, a, :],
                                  (v_cur if b else v_mid)[p][:, h0:h0 + 2, :].rearrange("p h d -> p (h d)"),
                                  start=True, stop=True)
                    last.then_inc(pv_done, 1)

                if cur:
                    scores(0)
                if nxt:
                    pe.wait_ge(xin_ld[1 - p], 16 * (hf + p + 1))
                    wait(pe, x1T_out, t - 1)
                    for k in range(CC):
                        last = nc.tensor.transpose(ps_x[:, k, :], xin[1 - p][:, k * P:(k + 1) * P], ident[:, :])
                    last.then_inc(xT_done, 1)
                if cur:
                    scores_t(0)
                    scores(1)
                if prv:
                    pe.wait_ge(att_done, t)
                    wait(pe, lg_out, t - 1)
                    for b in range(2):
                        last = nc.tensor.transpose(ps_m[:, b * P:(b + 1) * P],
                                                   att[:, b, :, :, :].rearrange("p c a d -> p (c a d)"),
                                                   ident[:, :])
                    last.then_inc(attT_done, 1)
                if nxt:
                    pe.wait_ge(xl_done, t + 2)
                    if isinstance(t, int) and t < 0:
                        pe.wait_ge(wlo_done, 2)
                    for m in range(2 * CC):
                        cols = slice(m * P, (m + 1) * P)
                        mm(ps_qk[:, m, :], bqk[:, cols], ones16[:, :], start=True, stop=False)
                        last = product(ps_qk[:, m, :], [(wa[0][:, k, cols], wa[1][:, k, cols]) for k in range(CC)],
                                       [(xT[0][:, k, :], xT[1][:, k, :]) for k in range(CC)], start=False)
                    last.then_inc(qk_done, 1)
                if cur:
                    less_maxima(0)
                if prv:
                    pe.wait_ge(al_done, t)
                    if isinstance(t, int):
                        pe.wait_ge(wlo_done, 4)
                    product(ps_m[:, 0:C], [tuple(attT[s][:, e, :, :].rearrange("p b q -> p (b q)") for s in range(2))
                                            for e in range(2)],
                            [(wp[0][:, e, :], wp[1][:, e, :]) for e in range(2)]).then_inc(proj_done, 1)
                if cur:
                    scores(2)
                    scores_t(1)
                    less_maxima(1)
                    scores(3)
                    values(0)
                    scores_t(2)
                    less_maxima(2)
                    values(1)
                    scores_t(3)
                    less_maxima(3)
                if nxt:
                    wait(pe, y_done, t)
                    product(ps_m[:, 0:C], [(xT[0][:, k, :], xT[1][:, k, :]) for k in range(CC)],
                            [(wa[0][:, k, 2 * C:3 * C], wa[1][:, k, 2 * C:3 * C]) for k in range(CC)])\
                        .then_inc(v_done, 1)
                if cur:
                    values(2)
                if prv:
                    pe.wait_ge(x1_done, t)
                    wait(pe, qkl_done, t + 2 if nxt else 0)
                    for k in range(CC):
                        last = nc.tensor.transpose(ps_x[:, k, :], x1[:, k * P:(k + 1) * P], ident[:, :])
                    last.then_inc(x1T_done, 1)
                if cur:
                    values(3)
                if prv:
                    pe.wait_ge(x1T_out, t)
                    wait(pe, v_out, t + 2 if nxt else 0)
                    for k in range(CC):
                        last = mm(ps_m[:, 0:E], x1T[:, k, :], wrT[:, k, :], start=k == 0, stop=k == CC - 1)
                    last.then_inc(lg_done, 1)

            walk_tokens(pe, body)

            pe.wait_ge(onehot_done, 1)
            oh = onehot[:, :, :].rearrange("p t e -> p (t e)")
            mm(ps[:, 0, 0:TILES * E], before[:, :], oh, start=True, stop=True)
            mm(ps[:, 1, 0:TILES * E], ones_b[:, :], oh, start=True, stop=True).then_inc(rank_done, 1)

            TURNS = 17

            def body3(j, p, hf, load, up, down, norm):
                if load:
                    pe.wait_ge(xa_ld[p], 16 * (hf + 2))
                    wait(pe, sl_done, j + 1)
                    for k in range(CC):
                        last = nc.tensor.transpose(ps_sx[p][:, k, :], xa[p][:, k * P:(k + 1) * P], ident[:, :])
                    last.then_inc(sT_done, 1)
                if up:
                    e = pe.value_load(expert[0:1, bass.ds(j + 1, 1)], min_val=0, max_val=E - 1)
                    pe.wait_ge(sl_done, j + 2)

                def weights(s, k, ic):
                    return w1s[s][:, bass.ds(e * CC + k, 1), ic * P:(ic + 1) * P].rearrange("p a i -> p (a i)")

                if down:
                    wait(pe, y2_done, j - 1)

                def output(first, last):
                    for n in range(first, last):
                        ic, (hs, ws) = n // 3, ((0, 0), (1, 0), (0, 1))[n % 3]
                        if n in (0, 3 * IC // 2):
                            pe.wait_ge(hl_done, 2 * j + 1 + (n > 0))
                        ins = mm(ps_y[p], h[p][hs][:, ic, :], wo[ws][:, ic, :], start=n == 0, stop=n == 3 * IC - 1)
                        if n == 3 * IC - 1:
                            ins.then_inc(ffn_done, 1)

                for ic in range(IC):
                    half, col = ic // (IC // 2), (ic % (IC // 2)) * P
                    if up and col == 0:
                        wait(pe, g_done, 2 * j - 1 + half)
                    for k in range(CC):
                        if up:
                            for n, (ws, ss) in enumerate(((0, 0), (1, 0), (0, 1))):
                                up_ins = mm(ps_h[1 - p][:, half, col:col + P], weights(ws, k, ic),
                                            sT[1 - p][ss][:, k, :], start=k + n == 0, stop=k == CC - 1 and n == 2)
                            if col == (IC // 2 - 1) * P and k == CC - 1:
                                up_ins.then_inc(h_done, 1)
                        if down:
                            g0 = ic * CC + k
                            output(g0 * TURNS // (IC * CC), (g0 + 1) * TURNS // (IC * CC))
                if down:
                    output(TURNS, 3 * IC)

            pe.wait_ge(slots_known, 1)
            pe.wait_ge(w1l_done, TILES)
            walk_slots(pe, body3)


_INS = ['L0_attn_x', 'L0_attn_W_attn', 'L0_attn_b_attn', 'L0_attn_W_proj', 'L0_attn_b_proj', 'L0_ffn_Wr',
        'L0_ffn_W1', 'L0_ffn_b1', 'L0_ffn_Wo', 'L0_ffn_bo', 'L0_ffn_gamma', 'L0_ffn_beta']
_OUTS = [((2, 2048, 256), 'float32')]


def kernel(**inputs):
    import numpy as _np
    import concourse.bacc as _bacc
    from concourse import mybir as _mybir
    from concourse.bass_utils import run_bass_kernel_spmd as _run

    nc = _bacc.Bacc("TRN2", target_bir_lowering=False, num_devices=1)
    arrays, args = {}, []
    for name in _INS:
        a = _np.ascontiguousarray(inputs[name])
        arrays[f"in_{name}_dram"] = a
        args.append(nc.dram_tensor(f"in_{name}_dram", a.shape, _mybir.dt.from_np(a.dtype), kind="ExternalInput").ap())
    for i, (shape, dtype) in enumerate(_OUTS):
        dt = _mybir.dt.from_np(_np.dtype(dtype))
        args.append(nc.dram_tensor(f"out_{i}_dram", shape, dt, kind="ExternalOutput").ap())
    attention_then_routed_ffn(nc, *args)
    r = _run(nc, [arrays], core_ids=[0])
    got = tuple(r.results[0][f"out_{i}_dram"] for i in range(len(_OUTS)))
    return got[0]
```

```python
import concourse.bass as bass
from concourse import mybir
from contextlib import ExitStack


def attention_then_routed_ffn(
    nc: bass.Bass,
    x: bass.AP,
    w_attn: bass.AP,
    b_attn: bass.AP,
    w_proj: bass.AP,
    b_proj: bass.AP,
    w_router: bass.AP,
    w1: bass.AP,
    b1: bass.AP,
    w_out: bass.AP,
    b_out: bass.AP,
    gamma: bass.AP,
    beta: bass.AP,
    out: bass.AP,
):
    f32, f16, bf16 = mybir.dt.float32, mybir.dt.float16, mybir.dt.bfloat16
    i32 = mybir.dt.int32
    ALU = mybir.AluOpType
    ACT = mybir.ActivationFunctionType
    AX = mybir.AxisListType

    P = 128
    B, T, C = x.shape
    E, _, I = w1.shape
    N = B * T
    HEADS = 16
    HD = C // HEADS
    BLK = 64
    SCALE = float(HD) ** -0.5
    TILES = N // P
    SEQ = T // P
    CC = C // P
    CH = HEADS // CC
    PAIRS = CH // 2
    UNITS_T = CC * 2
    IC = I // P
    SLOT_TILES = TILES + E - 1
    REGION = N + P
    SLOTS = E * REGION + (E - 1) * P
    W_UP = 64.0
    W_DOWN = 1.0 / W_UP
    EPS_OUTER, EPS_FFN = 1e-5, 1e-12
    MASKED = -1e30
    ROW = C + 1
    NO_TOKEN = 1 << 20
    UNITS = E * CC
    assert UNITS * 2 == TILES and TILES % 2 == 0 and SLOT_TILES % 2 == 1

    x_rows = x.rearrange("b (t p) c -> (b t) p c", p=P)
    out_rows = out.rearrange("b t c -> (b t) c")
    w1_units = w1.rearrange("e (k p) i -> (e k) p i", p=P)
    slots = nc.dram_tensor("slots", [SLOTS, ROW], f32, kind="Internal").ap()

    def wait(eng, sem, count):
        if not isinstance(count, int) or count > 0:
            eng.wait_ge(sem, count)

    ctx = ExitStack()
    with ctx:
        def sb(name, shape, dt):
            return ctx.enter_context(nc.sbuf_tensor(name, shape, dt))

        def sem(name):
            return ctx.enter_context(nc.semaphore(name))

        wa_in = sb("wa_in", [P, CC, 3 * C], f32)
        wp_in = sb("wp_in", [P, 2, C], f32)
        wo_in = sb("wo_in", [P, IC, C], f32)
        bqk_in = sb("bqk_in", [1, 2 * C], f32)
        wa = [sb(f"wa_{s}", [P, CC, 3 * C], f16) for s in ("hi", "lo")]
        wp = [sb(f"wp_{s}", [P, CC, C], f16) for s in ("hi", "lo")]
        wo = [sb(f"wo_{s}", [P, IC, C], f16) for s in ("hi", "lo")]
        w1s = [sb(f"w1_{s}", [P, UNITS, I], f16) for s in ("hi", "lo")]
        w1_in = sb("w1_in", [P, I], f32)
        bqk = sb("bqk", [64, 2 * C], f16)
        ones16 = sb("ones16", [64, P], f16)
        bv = sb("bv", [P, C], f32)
        bp = sb("bp", [P, C], f32)
        bo = sb("bo", [P, C], f32)
        gam = sb("gam", [P, C], f32)
        bet = sb("bet", [P, C], f32)
        wr_in = sb("wr_in", [E, C], f32)
        wrT = sb("wrT", [P, CC, E], f32)
        b1_in = sb("b1_in", [E * IC, P], f32)
        b1T = sb("b1T", [P, E * IC], f32)
        ident = sb("ident", [P, P], f32)
        ident_b = sb("ident_b", [P, P], bf16)
        mask_q = sb("mask_q", [P, 2, P], bf16)
        mask_k = sb("mask_k", [P, 2, 2, P], bf16)
        eye64 = sb("eye64", [P, BLK], bf16)
        band = sb("band", [P, CH], f32)
        before = sb("before", [P, P], bf16)
        ones_b = sb("ones_b", [P, P], bf16)
        fill = sb("fill", [P, ROW], f32)
        power, zero, eps_outer, eps_ffn = (sb(n, [P, 1], f32) for n in ("power", "zero", "eps_outer", "eps_ffn"))

        xin = [sb(f"xin{k}", [P, C], f32) for k in range(2)]
        xres = [sb(f"xres{k}", [P, C], f32) for k in range(2)]
        xT = [sb(f"xT_{s}", [P, CC, P], f16) for s in ("hi", "lo")]
        q = sb("q", [P, 2, CC, 2, BLK], f16)
        qbd = [sb(f"qbd{k}", [P, 2, CC, 2, CH, BLK], f16) for k in range(2)]
        k_ = [sb(f"k{k}", [P, 2, CC, BLK + P], f16) for k in range(2)]
        v_cur = [sb(f"v_cur{k}", [P, HEADS, HD + 1], f32) for k in range(2)]
        v_mid = [sb(f"v_mid{k}", [P, HEADS, HD + 1], f32) for k in range(2)]
        mx = [sb(f"mx{k}", [P, PAIRS], f32) for k in range(2)]
        diag = [sb(f"diag{k}", [P, 2, PAIRS, BLK], bf16) for k in range(2)]
        probs = [sb(f"probs{u}", [P, PAIRS, P], f32) for u in range(UNITS_T)]
        rden = sb("rden", [P, CC, 2 * PAIRS], f32)
        att = sb("att", [P, 2, CC, PAIRS, HD], f32)
        attT = [sb(f"attT_{s}", [P, 2, 2, BLK], f16) for s in ("hi", "lo")]
        y = sb("y", [P, C], f32)
        stats = sb("stats", [P, 6], f32)
        meanvar = sb("meanvar", [P, 2], f32)
        veps = sb("veps", [P, 1], f32)
        rstd = sb("rstd", [P, 1], f32)
        x1T = sb("x1T", [P, CC, P], f32)
        row = [sb(f"row{k}", [P, ROW], f32) for k in range(2)]
        two_tiles = sb("two_tiles", [P, 1], f32)
        logits = sb("logits", [P, E], f32)
        desc = sb("desc", [P, E], f32)
        top = sb("top", [P, 1], f32)
        pick = sb("pick", [P, E], f32)
        first = sb("first", [P, 1], f32)
        onehot = sb("onehot", [P, E], bf16)
        next_slot = sb("next_slot", [P, E], f32)
        place = sb("place", [P, E], f32)
        placed = sb("placed", [P, E], f32)
        slot_f = sb("slot_f", [P, 1], f32)
        slot_of = [sb(f"slot_of{k}", [P, 1], i32) for k in range(2)]

        region_at = sb("region_at", [1, E], f32)
        table_in = sb("table_in", [1, 1], f32)
        pad_at = sb("pad_at", [1, E], i32)
        total = sb("total", [1, E], f32)
        thresholds = sb("thresholds", [1, E, TILES], f32)
        over = sb("over", [1, E, TILES], f32)
        ntiles = sb("ntiles", [1, E], f32)
        ones_e = sb("ones_e", [1, E], f32)
        tend = sb("tend", [1, E], f32)
        skip = sb("skip", [1, E], f32)
        tile_no = sb("tile_no", [1, SLOT_TILES, E], f32)
        past = sb("past", [1, SLOT_TILES, E], f32)
        skipped = sb("skipped", [1, SLOT_TILES, E], f32)
        offset = sb("offset", [1, SLOT_TILES], f32)
        base_f = sb("base_f", [1, SLOT_TILES], f32)
        base = sb("base", [1, SLOT_TILES], i32)
        expert_f = sb("expert_f", [1, SLOT_TILES], f32)
        expert = sb("expert", [1, SLOT_TILES], i32)

        xa = [sb(f"xa{k}", [P, C], f32) for k in range(2)]
        xr = [sb(f"xr{k}", [P, C], f32) for k in range(2)]
        token = [sb(f"token{k}", [P, 2], f32) for k in range(2)]
        token_i = [sb(f"token_i{k}", [P, 1], i32) for k in range(2)]
        sT = [[sb(f"sT{k}_{s}", [P, CC, P], f16) for s in ("hi", "lo")] for k in range(2)]
        g = [sb(f"g{k}", [P, IC, P], f32) for k in range(2)]
        h = [[sb(f"h{k}_{s}", [P, IC, P], f16) for s in ("hi", "lo")] for k in range(2)]
        room = [qbd[k][:, :, :, :, :, :].rearrange("p s c b h q -> p (s c b h q)").bitcast(f32) for k in range(2)]
        xbo, xbe, fin = ([room[k][:, n * C:(n + 1) * C] for k in range(2)] for n in range(3))
        y2, ng, z = (room[n % 2][:, (3 + n // 2) * C:(4 + n // 2) * C] for n in range(3))
        stats_a = sb("stats_a", [P, 6], f32)
        stats_b = sb("stats_b", [P, 6], f32)
        mv_a = sb("mv_a", [P, 2], f32)
        mv_b = sb("mv_b", [P, 2], f32)
        ve_a = sb("ve_a", [P, 1], f32)
        ve_b = sb("ve_b", [P, 1], f32)
        rs_a = sb("rs_a", [P, 1], f32)
        rs_b = sb("rs_b", [P, 1], f32)

        ps = ctx.enter_context(nc.psum_tensor("ps", [P, 8, 512], f32))
        ps_x = ps[:, 0, 0:CC * P].rearrange("p (k t) -> p k t", k=CC)
        ps_qk = ps[:, 0, :].rearrange("p (m t) -> p m t", m=2 * CC)
        ps_m = ps[:, 1, :]
        ps_rank = ps_m[:, C:C + 2 * E]
        ps_aT = ps_m[:, 0:C].rearrange("p (b e q) -> p e b q", b=2, e=2)
        ps_s = [ps[:, 2 + k, :] for k in range(2)]
        ps_t = [ps[:, 4 + k, :] for k in range(2)]
        ps_o = ps[:, 6:6 + CC, 0:2 * PAIRS * 2 * (HD + 1)].rearrange("p c (n o) -> p c n o", o=2 * (HD + 1))
        ps_h = [ps[:, 2 * k:2 * k + 2, :] for k in range(2)]
        ps_y = [ps[:, 4 + k, 0:C] for k in range(2)]
        ps_sx = [ps[:, 6 + k, 0:CC * P].rearrange("p (k t) -> p k t", k=CC) for k in range(2)]

        qkv_w_ld, attn_w_ld, ffn_w_ld = sem("qkv_w_ld"), sem("attn_w_ld"), sem("ffn_w_ld")
        xin_ld = [sem(f"xin_ld{k}") for k in range(2)]
        xres_ld = [sem(f"xres_ld{k}") for k in range(2)]
        w1_ld, fill_st, pad_st, pad2_st = sem("w1_ld"), sem("fill_st"), sem("pad_st"), sem("pad2_st")
        disp_st = [sem(f"disp_st{k}") for k in range(2)]
        consts_done, consts_step = sem("consts_done"), sem("consts_step")
        qbdh_done, qbd_done, masks_done = sem("qbdh_done"), sem("qbd_done"), sem("masks_done")
        whi_done, wlo_done = sem("whi_done"), sem("wlo_done")
        setupT_done, setupT_out = sem("setupT_done"), sem("setupT_out")
        xT_done, xh_done, xl_done = sem("xT_done"), sem("xh_done"), sem("xl_done")
        qk_done, qkh_done, qkl_done = sem("qk_done"), sem("qkh_done"), sem("qkl_done")
        kcar_done = sem("kcar_done")
        v_done, v_out, vlow_done, vhigh_done = sem("v_done"), sem("v_out"), sem("vlow_done"), sem("vhigh_done")
        s_done, mx_done, diaglow_done, diag_done, st_done = sem("s_done"), sem("mx_done"), sem("diaglow_done"), sem("diag_done"), sem("st_done")
        exp_done, pv_done = sem("exp_done"), sem("pv_done")
        rden_done, att_done, attT_done = sem("rden_done"), sem("att_done"), sem("attT_done")
        ah_done, al_done = sem("ah_done"), sem("al_done")
        proj_done, xrb_done, y_done = sem("proj_done"), sem("xrb_done"), sem("y_done")
        bn_done, mv_done, rstd_done = sem("bn_done"), sem("mv_done"), sem("rstd_done")
        x1_done, number_done, x1T_done, x1T_out = sem("x1_done"), sem("number_done"), sem("x1T_done"), sem("x1T_out")
        lg_done, lg_out = sem("lg_done"), sem("lg_out")
        w1h_done, w1l_done = sem("w1h_done"), sem("w1l_done")
        top_done, pick_done, first_done, onehot_done = sem("top_done"), sem("pick_done"), sem("first_done"), sem("onehot_done")
        rank_done, place_done, next_done, placed_done = sem("rank_done"), sem("place_done"), sem("next_done"), sem("placed_done")
        slotf_done, slot_done, pads_known = sem("slotf_done"), sem("slot_done"), sem("pads_known")
        table_step, bases_known, slots_known = sem("table_step"), sem("bases_known"), sem("slots_known")
        number_out = sem("number_out")
        xa_ld = [sem(f"xa_ld{k}") for k in range(2)]
        xr_ld = [sem(f"xr_ld{k}") for k in range(2)]
        token_ld = [sem(f"token_ld{k}") for k in range(2)]
        sT_done, sh_done, sl_done = sem("sT_done"), sem("sh_done"), sem("sl_done")
        h_done, g_done, hh_done, hl_done = sem("h_done"), sem("g_done"), sem("hh_done"), sem("hl_done")
        ffn_done, y2_done, bna_done, mva_done = sem("ffn_done"), sem("y2_done"), sem("bna_done"), sem("mva_done")
        rsa_done, ng_done, z_done = sem("rsa_done"), sem("ng_done"), sem("z_done")
        bnb_done, mvb_done, rsb_done, fin_done = sem("bnb_done"), sem("mvb_done"), sem("rsb_done"), sem("fin_done")
        veps_done, vea_done, veb_done = sem("veps_done"), sem("vea_done"), sem("veb_done")
        xbo_done, xbe_done = sem("xbo_done"), sem("xbe_done")
        out_st = [sem(f"out_st{k}") for k in range(2)]

        QKV_LOADS, ATTN_LOADS, FFN_LOADS = 2, 4, 6
        N_CONSTS = 1

        def apart(eng):
            eng.wait_ge(attn_w_ld, 16 * ATTN_LOADS)

        def variant(t):
            if isinstance(t, int):
                return min(t % SEQ, 1)
            return (t % SEQ + (SEQ - 1)) // SEQ

        def walk_tokens(eng, body):
            body(-1, 1, -1, True, False, False, False)
            body(0, 0, 0, True, True, False, False)
            body(1, 1, 0, True, True, True, False)
            for t in range(2, 5):
                body(t, t % 2, t // 2, True, True, True, True)
            with eng.Fori(0, (TILES - 6) // 2) as i:
                body(2 * i + 5, 1, i + 2, True, True, True, True)
                body(2 * i + 6, 0, i + 3, True, True, True, True)
            body(TILES - 1, 1, (TILES - 1) // 2, False, True, True, True)
            body(TILES, 0, TILES // 2, False, False, True, True)
            body(TILES + 1, 1, TILES // 2, False, False, False, True)

        def walk_slots(eng, body):
            body(-2, 0, -1, True, False, False, False)
            body(-1, 1, -1, True, True, False, False)
            body(0, 0, 0, True, True, True, False)
            body(1, 1, 0, True, True, True, True)
            body(2, 0, 1, True, True, True, True)
            with eng.Fori(0, (SLOT_TILES - 5) // 2) as i:
                body(2 * i + 3, 1, i + 1, True, True, True, True)
                body(2 * i + 4, 0, i + 2, True, True, True, True)
            last = SLOT_TILES - 1
            body(last - 1, 1, (last - 1) // 2, False, True, True, True)
            body(last, 0, last // 2, False, False, True, True)
            body(last + 1, 1, (last + 1) // 2, False, False, False, True)

        block = ctx.enter_context(nc.Block())

        @block.sync
        def _(sp):
            sp.dma_start(xin[0][:, :], x_rows[0]).then_inc(xin_ld[0], 16)
            sp.dma_start(wa_in[:, :, :], w_attn.rearrange("(k p) n -> p k n", p=P)).then_inc(qkv_w_ld, 16)
            sp.dma_start(xin[1][:, :], x_rows[1]).then_inc(xin_ld[1], 16)
            sp.dma_start(bqk_in[:, :], b_attn[0:2 * C].unsqueeze(0)).then_inc(qkv_w_ld, 16)
            sp.dma_start(bv[:, :], b_attn[2 * C:3 * C].unsqueeze(0).broadcast_to([P, C])).then_inc(attn_w_ld, 16)
            for o in range(2):
                sp.dma_start(wp_in[:, o, :], w_proj.rearrange("(n o d) c -> o n d c", o=2, d=HD)[o])\
                    .then_inc(attn_w_ld, 16)
            sp.dma_start(bp[:, :], b_proj.unsqueeze(0).broadcast_to([P, C])).then_inc(attn_w_ld, 16)

            sp.wait_ge(consts_done, N_CONSTS)
            sp.dma_start(slots[E * REGION:SLOTS, :].rearrange("(j p) c -> p j c", p=P),
                         fill[:, :].unsqueeze(1).broadcast_to([P, E - 1, ROW])).then_inc(fill_st, 16)

            def body(t, p, hf):
                if not isinstance(t, int) or t + 2 < TILES:
                    wait(sp, xT_done, t + 1)
                    sp.dma_start(xin[p][:, :], x_rows[t + 2]).then_inc(xin_ld[p], 16)
                wait(sp, y_done, t - 1)
                sp.dma_start(xres[p][:, :], x_rows[t]).then_inc(xres_ld[p], 16)
                if p == 0:
                    wait(sp, w1l_done, 2 * hf)
                    sp.dma_start(w1_in[:, :], w1_units[hf]).then_inc(w1_ld, 16)

            for t in range(3):
                body(t, t % 2, t // 2)
            with sp.Fori(0, (TILES - 6) // 2) as i:
                body(2 * i + 3, 1, i + 1)
                body(2 * i + 4, 0, i + 2)
            for t in range(TILES - 3, TILES):
                body(t, t % 2, t // 2)

            sp.wait_ge(pads_known, 1)
            for e in range(E // 2):
                at = sp.value_load(pad_at[0:1, e:e + 1], min_val=0, max_val=SLOTS - P)
                sp.dma_start(slots[bass.ds(at, P), :], fill[:, :]).then_inc(pad_st, 16)
            sp.wait_ge(bases_known, 1)

            def rows_of(j, first, last):
                at = sp.value_load(base[0:1, bass.ds(j, 1)], min_val=0, max_val=SLOTS - P)
                return slots[bass.ds(at, P), first:last]

            sp.wait_ge(fill_st, 16)
            sp.wait_ge(pad_st, 16 * (E // 2))
            sp.wait_ge(pad2_st, 16 * (E // 2))
            for k in range(2):
                sp.wait_ge(disp_st[k], 16 * TILES // 2)
            sp.dma_start(xa[0][:, :], rows_of(0, 0, C)).then_inc(xa_ld[0], 16)
            sp.dma_start(xa[1][:, :], rows_of(1, 0, C)).then_inc(xa_ld[1], 16)
            sp.dma_start(xr[0][:, :], rows_of(0, 0, C)).then_inc(xr_ld[0], 16)
            sp.wait_ge(sT_done, 1)
            sp.dma_start(xa[0][:, :], rows_of(2, 0, C)).then_inc(xa_ld[0], 16)

            def loads(j, p, hf):
                if not isinstance(j, int) or j + 3 < SLOT_TILES:
                    src = rows_of(j + 3, 0, C)
                    sp.wait_ge(sT_done, j + 2)
                    sp.dma_start(xa[1 - p][:, :], src).then_inc(xa_ld[1 - p], 16)
                if not isinstance(j, int) or j + 1 < SLOT_TILES:
                    src = rows_of(j + 1, 0, C)
                    wait(sp, xbe_done, j)
                    sp.dma_start(xr[1 - p][:, :], src).then_inc(xr_ld[1 - p], 16)
                src = rows_of(j, C - 1, ROW)
                wait(sp, number_out, j - 1)
                sp.dma_start(token[p][:, :], src).then_inc(token_ld[p], 16)

            for j in range(3):
                loads(j, j % 2, j // 2)
            with sp.Fori(0, (SLOT_TILES - 7) // 2) as i:
                loads(2 * i + 3, 1, i + 1)
                loads(2 * i + 4, 0, i + 2)
            for j in range(SLOT_TILES - 4, SLOT_TILES):
                loads(j, j % 2, j // 2)
            sp.wait_ge(out_st[0], 16 * ((SLOT_TILES + 1) // 2))
            sp.wait_ge(out_st[1], 16 * (SLOT_TILES // 2))

        @block.gpsimd
        def _(pool):
            step = [0]

            def link(ins):
                step[0] += 1
                ins.then_inc(consts_step, 1)
                pool.wait_ge(consts_step, step[0])

            link(nc.gpsimd.memset(ident[:, :], 0.0))
            link(nc.gpsimd.affine_select(out=ident[:, :], in_=ident[:, :], compare_op=ALU.not_equal, fill=1.0,
                                         base=0, pattern=[[-1, P]], channel_multiplier=1))
            link(nc.gpsimd.tensor_copy(ident_b[:, :], ident[:, :]))
            link(nc.gpsimd.memset(fill[:, :], 0.0))
            link(nc.gpsimd.memset(fill[:, C:ROW], float(NO_TOKEN)))
            link(nc.gpsimd.memset(band[:, :], 1.0))
            link(nc.gpsimd.affine_select(out=band[:, :], in_=band[:, :], compare_op=ALU.is_ge, fill=0.0,
                                         base=0, pattern=[[-HD, CH]], channel_multiplier=1))
            link(nc.gpsimd.affine_select(out=band[:, :], in_=band[:, :], compare_op=ALU.is_ge, fill=0.0,
                                         base=HD - 1, pattern=[[HD, CH]], channel_multiplier=-1))
            nc.gpsimd.memset(bqk[:, :], 0.0)
            nc.gpsimd.memset(ones16[:, :], 1.0)
            link(nc.gpsimd.memset(mask_q[:, :, :], 0.0))
            for e in range(2):
                r = slice(BLK * e, BLK * e + BLK)
                for sign, base in ((1, 0), (-1, BLK)):
                    link(nc.gpsimd.affine_select(
                        out=mask_q[r, :, :], in_=mask_q[r, :, :], compare_op=ALU.is_ge, fill=MASKED,
                        base=base, pattern=[[0, 2], [sign, P]], channel_multiplier=-sign))
            nc.gpsimd.memset(mask_q[:, 0, 0:BLK], MASKED)
            nc.gpsimd.tensor_tensor(eye64[:, :], ident[:, 0:BLK], ident[:, BLK:P], ALU.add)
            nc.gpsimd.memset(mask_k[:, :, :, :], -1.0).then_inc(masks_done, 1)
            for k in range(2):
                nc.gpsimd.memset(v_cur[k][:, :, :], 1.0)
                nc.gpsimd.memset(v_mid[k][:, :, :], 1.0)
            nc.gpsimd.memset(k_[0][:, :, :, 0:BLK], 0.0)
            link(nc.gpsimd.memset(ones_b[:, :], 1.0))
            link(nc.gpsimd.affine_select(out=before[:, :], in_=ones_b[:, :], compare_op=ALU.is_ge, fill=0.0,
                                         base=-1, pattern=[[1, P]], channel_multiplier=-1))
            for k in range(2):
                nc.gpsimd.iota(row[k][:, C:ROW], pattern=[[0, 1]], base=k * P, channel_multiplier=1,
                               allow_small_or_imprecise_dtypes=True)
            for start in (next_slot[:, :], region_at[:, :]):
                nc.gpsimd.iota(start, pattern=[[REGION, E]], base=0, channel_multiplier=0,
                               allow_small_or_imprecise_dtypes=True)
            nc.gpsimd.iota(desc[:, :], pattern=[[-1, E]], base=E, channel_multiplier=0,
                           allow_small_or_imprecise_dtypes=True)
            nc.gpsimd.memset(ones_e[:, :], 1.0)
            for const, value in ((two_tiles, 2.0 * P), (power, -0.5), (zero, 0.0), (eps_outer, EPS_OUTER), (eps_ffn, EPS_FFN)):
                nc.gpsimd.memset(const[:, :], value)
            nc.gpsimd.iota(thresholds[:, :, :], pattern=[[0, E], [P, TILES]], base=0, channel_multiplier=0,
                           allow_small_or_imprecise_dtypes=True)
            nc.gpsimd.iota(tile_no[:, :, :], pattern=[[1, SLOT_TILES], [0, E]], base=0,
                           channel_multiplier=0, allow_small_or_imprecise_dtypes=True).then_inc(consts_done, 1)

            pool.wait_ge(attn_w_ld, 16 * ATTN_LOADS)

            def body(t, p, hf, nxt, cur, prv, old):
                if cur:
                    pool.wait_ge(qkl_done, t + 1)
                    wait(pool, st_done, 4 * t)
                    nc.gpsimd.tensor_tensor(k_[1 - p][:, :, :, 0:BLK], k_[p][:, :, :, P:P + BLK],
                                            zero[:, :].unsqueeze(2).unsqueeze(3).broadcast_to([P, 2, CC, BLK]),
                                            ALU.add)\
                        .then_inc(kcar_done, 1)

                def diagonals(u):
                    pool.wait_ge(mx_done, 4 * t + u + 1)
                    wait(pool, st_done, 4 * t + u - 1)
                    wait(pool, diag_done, 4 * t + u)
                    for e in range(2):
                        r = slice(BLK * e, BLK * e + BLK)
                        if e == 1:
                            pool.wait_ge(diaglow_done, 4 * t + u + 1)
                            if u == 0:
                                wait(pool, disp_st[1 - p], 16 * (hf + p - 1))
                        nc.gpsimd.tensor_tensor(
                            diag[u % 2][r, e, :, :], eye64[r, :].unsqueeze(1).broadcast_to([BLK, PAIRS, BLK]),
                            mx[u % 2][r, :].unsqueeze(2).broadcast_to([BLK, PAIRS, BLK]), ALU.mult)\
                            .then_inc(diag_done if e else diaglow_done, 1)

                if cur:
                    diagonals(0)
                    pool.wait_ge(diag_done, 4 * t + 1)
                if prv:
                    pool.wait_ge(xres_ld[1 - p], 16 * (hf + p))
                    nc.gpsimd.tensor_tensor(xres[1 - p][:, :], xres[1 - p][:, :], bp[:, :], ALU.add)\
                        .then_inc(xrb_done, 1)
                if cur:
                    diagonals(1)
                    diagonals(2)
                    diagonals(3)
                    pool.wait_ge(diag_done, 4 * t + 4)
                if prv:
                    pool.wait_ge(mv_done, t)
                    wait(pool, x1_done, t - 1)
                    nc.gpsimd.tensor_tensor(veps[:, :], meanvar[:, 1:2], eps_outer[:, :], ALU.add)\
                        .then_inc(veps_done, 1)
                    pool.wait_ge(veps_done, t)
                    nc.gpsimd.tensor_tensor(rstd[:, :], veps[:, :], power[:, :], ALU.pow).then_inc(rstd_done, 1)
                if prv and not (isinstance(t, int) and t < 3):
                    wait(pool, disp_st[1 - p], 16 * (hf + p - 1))
                    wait(pool, number_done, t - 3)
                    nc.gpsimd.tensor_tensor(row[1 - p][:, C:ROW], row[1 - p][:, C:ROW], two_tiles[:, :], ALU.add)\
                        .then_inc(number_done, 1)
                if old:
                    if not prv:
                        pool.wait_ge(number_done, t - 3)
                    apart(pool)
                    pool.wait_ge(slot_done, t - 1)
                    pool.wait_ge(x1_done, t - 1)
                    nc.gpsimd.indirect_dma_start(
                        out=slots, out_offset=bass.IndirectOffsetOnAxis(ap=slot_of[p][:, :], axis=0),
                        in_=row[p][:, :], in_offset=None, bounds_check=SLOTS - 1, oob_is_err=False)\
                        .then_inc(disp_st[p], 16)

            walk_tokens(pool, body)
            pool.wait_ge(ffn_w_ld, 16 * FFN_LOADS)

            def body3(j, p, hf, load, up, down, norm):
                if norm:
                    pool.wait_ge(mva_done, j)
                    wait(pool, z_done, j - 1)
                    nc.gpsimd.tensor_tensor(ve_a[:, :], mv_a[:, 1:2], eps_ffn[:, :], ALU.add)\
                        .then_inc(vea_done, 1)
                    pool.wait_ge(vea_done, j)
                    nc.gpsimd.tensor_tensor(rs_a[:, :], ve_a[:, :], power[:, :], ALU.pow)\
                        .then_inc(rsa_done, 1)
                if down:
                    pool.wait_ge(xr_ld[p], 16 * (hf + 1))
                    wait(pool, y2_done, j - 1)
                    nc.gpsimd.tensor_tensor(xbo[p], xr[p][:, :], bo[:, :], ALU.add).then_inc(xbo_done, 1)
                    wait(pool, z_done, j - 1)
                    nc.gpsimd.tensor_tensor(xbe[p], xr[p][:, :], bet[:, :], ALU.add).then_inc(xbe_done, 1)
                if norm:
                    pool.wait_ge(mvb_done, j)
                    wait(pool, fin_done, j - 1)
                    nc.gpsimd.tensor_tensor(ve_b[:, :], mv_b[:, 1:2], eps_outer[:, :], ALU.add)\
                        .then_inc(veb_done, 1)
                    pool.wait_ge(veb_done, j)
                    nc.gpsimd.tensor_tensor(rs_b[:, :], ve_b[:, :], power[:, :], ALU.pow)\
                        .then_inc(rsb_done, 1)
                if norm:
                    apart(pool)
                    pool.wait_ge(fin_done, j)
                    pool.wait_ge(number_out, j)
                    nc.gpsimd.indirect_dma_start(
                        out=out_rows,
                        out_offset=bass.IndirectOffsetOnAxis(ap=token_i[1 - p][:, :], axis=0),
                        in_=fin[1 - p], in_offset=None, bounds_check=N - 1, oob_is_err=False)\
                        .then_inc(out_st[1 - p], 16)

            walk_slots(pool, body3)

        @block.scalar
        def _(act):
            for dst, src in ((wr_in[:, :], w_router), (b1_in[:, :], b1.rearrange("e (k p) -> (e k) p", p=P)),
                             (wo_in[:, :, :], w_out.rearrange("(k p) n -> p k n", p=P)),
                             (bo[:, :], b_out.unsqueeze(0).broadcast_to([P, C])),
                             (gam[:, :], gamma.unsqueeze(0).broadcast_to([P, C])),
                             (bet[:, :], beta.unsqueeze(0).broadcast_to([P, C]))):
                act.dma_start(dst, src).then_inc(ffn_w_ld, 16)
            act.wait_ge(masks_done, 1)
            for e in range(2):
                r = slice(BLK * (1 - e), BLK * (1 - e) + BLK)
                nc.scalar.activation(mask_k[r, e, :, :], mask_q[r, :, :], ACT.Copy)
                for k in range(2):
                    nc.scalar.activation(diag[k][r, e, :, :],
                                         eye64[r, :].unsqueeze(1).broadcast_to([BLK, PAIRS, BLK]), ACT.Copy)
            act.wait_ge(qkv_w_ld, 16 * QKV_LOADS)
            nc.scalar.activation(wa[0][:, :, :], wa_in[:, :, :], ACT.Copy, scale=W_UP).then_inc(whi_done, 1)
            act.wait_ge(consts_done, N_CONSTS)
            nc.scalar.activation(bqk[0:1, :], bqk_in[:, :], ACT.Copy, scale=W_UP).then_inc(whi_done, 1)

            def later_weights():
                act.wait_ge(setupT_done, 1)
                nc.scalar.activation(wrT[:, :, :], ps[:, 1, 0:CC * E].rearrange("p (k e) -> p k e", k=CC), ACT.Copy)
                nc.scalar.activation(b1T[:, :], ps[:, 1, P:P + E * IC], ACT.Copy).then_inc(setupT_out, 1)
                act.wait_ge(attn_w_ld, 16 * ATTN_LOADS)
                nc.scalar.activation(wp[0][:, :, :], wp_in[:, :, :], ACT.Copy, scale=W_UP).then_inc(whi_done, 1)
                act.wait_ge(ffn_w_ld, 16 * FFN_LOADS)
                nc.scalar.activation(wo[0][:, :, :], wo_in[:, :, :], ACT.Copy, scale=W_UP).then_inc(whi_done, 1)

            def body(t, p, hf, nxt, cur, prv, old):
                if old:
                    act.wait_ge(lg_done, t - 1)
                    wait(act, onehot_done, t - 2)
                    nc.scalar.activation(logits[:, :], ps_m[:, 0:E], ACT.Copy).then_inc(lg_out, 1)
                if nxt:
                    act.wait_ge(xT_done, t + 2)
                    wait(act, v_done, t + 1)
                    nc.scalar.activation(xT[0][:, :, :], ps_x, ACT.Copy).then_inc(xh_done, 1)
                if prv:
                    act.wait_ge(attT_done, t)
                    wait(act, proj_done, t - 1)
                    nc.scalar.activation(attT[0][:, :, :, :], ps_aT, ACT.Copy).then_inc(ah_done, 1)
                    piece, cols = hf + p - 1, slice((1 - p) * I // 2, (2 - p) * I // 2)
                    act.wait_ge(w1_ld, 16 * (hf + p))
                    nc.scalar.activation(w1s[0][:, piece, cols], w1_in[:, cols], ACT.Copy, scale=W_UP)\
                        .then_inc(w1h_done, 1)
                if nxt:
                    act.wait_ge(qk_done, t + 2)
                    wait(act, st_done, 4 * t)
                    wait(act, kcar_done, t)
                    nc.scalar.activation(k_[1 - p][:, 0, :, BLK:BLK + P], ps_qk[:, CC:2 * CC, :], ACT.Copy,
                                         scale=W_DOWN)
                    nc.scalar.activation(q[:, 0, :, :, :].rearrange("p c b q -> p c (b q)"), ps_qk[:, 0:CC, :],
                                         ACT.Copy, scale=W_DOWN).then_inc(qkh_done, 1)
                if isinstance(t, int) and t < 0:
                    later_weights()

                def spread(first, last):
                    for n in range(first, last):
                        ins = nc.scalar.activation(
                            qbd[1 - p][:, 0, :, :, n, :].rearrange("p c b q -> p (c b) q"),
                            q[:, 0, :, :, :].rearrange("p c b q -> p (c b) q"), ACT.Copy, scale=band[:, n:n + 1])
                    if last == CH:
                        ins.then_inc(qbdh_done, 1)

                def exps(u):
                    act.wait_ge(st_done, 4 * t + u + 1)
                    wait(act, pv_done, 4 * t + u - 3)
                    nc.scalar.activation(probs[u][:, :, :], ps_t[u % 2].rearrange("p (a q) -> p a q", a=PAIRS),
                                         ACT.Exp, scale=SCALE).then_inc(exp_done, 1)

                if cur:
                    exps(0)
                    act.wait_ge(v_out, t + 1)
                    wait(act, pv_done, 4 * t)
                    nc.scalar.activation(v_mid[1 - p][0:BLK, :, 0:HD], v_cur[p][BLK:P, :, 0:HD], ACT.Copy)\
                        .then_inc(vlow_done, 1)
                if nxt:
                    act.wait_ge(qkh_done, t + 2)
                    spread(0, 3)
                if cur:
                    exps(1)
                if nxt:
                    spread(3, 6)
                if cur:
                    exps(2)
                if nxt:
                    spread(6, CH)
                if cur:
                    exps(3)
                if nxt:
                    act.wait_ge(v_out, t + 2)
                    nc.scalar.activation(v_mid[1 - p][BLK:P, :, 0:HD], v_cur[1 - p][0:BLK, :, 0:HD], ACT.Copy)\
                        .then_inc(vhigh_done, 1)
                if prv:
                    act.wait_ge(x1T_done, t)
                    wait(act, lg_done, t - 1)
                    nc.scalar.activation(x1T[:, :, :], ps_x, ACT.Copy).then_inc(x1T_out, 1)

            walk_tokens(act, body)

            def body3(j, p, hf, load, up, down, norm):
                if load:
                    act.wait_ge(sT_done, j + 3)
                    wait(act, h_done, 2 * j + 2)
                    nc.scalar.activation(sT[p][0][:, :, :], ps_sx[p], ACT.Copy).then_inc(sh_done, 1)
                if up:
                    e = act.value_load(expert[0:1, bass.ds(j + 1, 1)], min_val=0, max_val=E - 1)
                    wait(act, hl_done, 2 * j)
                    for half in range(2):
                        act.wait_ge(h_done, 2 * j + 3 + half)
                        ics = range(half * IC // 2, (half + 1) * IC // 2)
                        for ic in ics:
                            col = (ic % (IC // 2)) * P
                            last = nc.scalar.activation(
                                g[1 - p][:, ic, :], ps_h[1 - p][:, half, col:col + P], ACT.Gelu,
                                bias=b1T[:, bass.ds(e * IC + ic, 1)], scale=W_DOWN)
                        last.then_inc(g_done, 1)
                        act.wait_ge(g_done, 2 * j + 3 + half)
                        wait(act, ffn_done, j)
                        nc.scalar.activation(h[1 - p][0][:, ics[0]:ics[-1] + 1, :],
                                             g[1 - p][:, ics[0]:ics[-1] + 1, :], ACT.Copy).then_inc(hh_done, 1)

            act.wait_ge(pads_known, 1)
            for e in range(E // 2, E):
                at = act.value_load(pad_at[0:1, e:e + 1], min_val=0, max_val=SLOTS - P)
                act.dma_start(slots[bass.ds(at, P), :], fill[:, :]).then_inc(pad2_st, 16)
            nc.scalar.activation(table_in[:, :], zero[0:1, :], ACT.Gelu)
            act.wait_ge(slots_known, 1)
            walk_slots(act, body3)

        @block.vector
        def _(dve):
            dve.wait_ge(whi_done, 1)
            nc.vector.scalar_tensor_tensor(wa[1][:, :, :], wa_in[:, :, :], W_UP, wa[0][:, :, :],
                                           ALU.mult, ALU.subtract).then_inc(wlo_done, 1)
            dve.wait_ge(whi_done, 2)
            nc.vector.scalar_tensor_tensor(bqk[32:33, :], bqk_in[:, :], W_UP, bqk[0:1, :],
                                           ALU.mult, ALU.subtract).then_inc(wlo_done, 1)

            def later_weights():
                dve.wait_ge(whi_done, 3)
                nc.vector.scalar_tensor_tensor(wp[1][:, :, :], wp_in[:, :, :], W_UP, wp[0][:, :, :],
                                               ALU.mult, ALU.subtract).then_inc(wlo_done, 1)
                dve.wait_ge(whi_done, 4)
                nc.vector.scalar_tensor_tensor(wo[1][:, :, :], wo_in[:, :, :], W_UP, wo[0][:, :, :],
                                               ALU.mult, ALU.subtract).then_inc(wlo_done, 1)

            def body(t, p, hf, nxt, cur, prv, old):
                def maxima(u):
                    dve.wait_ge(s_done, 4 * t + u + 1)
                    wait(dve, diag_done, 4 * t + u - 1)
                    nc.vector.tensor_reduce(mx[u % 2][:, :], ps_s[u % 2].rearrange("p (a k) -> p a k", k=P),
                                            AX.X, ALU.max).then_inc(mx_done, 1)

                if prv:
                    dve.wait_ge(pv_done, 4 * t)
                    wait(dve, att_done, t - 1)
                    for e in range(2):
                        r, one = slice(BLK * e, BLK * e + BLK), e * (HD + 1) + HD
                        last = nc.vector.reciprocal(rden[r, :, :], ps_o[r, :, :, one])
                    last.then_inc(rden_done, 1)
                    dve.wait_ge(rden_done, t)
                    wait(dve, attT_done, t - 1)
                    for e in range(2):
                        r, own = slice(BLK * e, BLK * e + BLK), e * (HD + 1)
                        for c in range(CC):
                            last = nc.vector.tensor_tensor(
                                att[r, :, c, :, :].rearrange("p b a d -> p b a d"),
                                ps_o[r, c, :, own:own + HD].rearrange("p (b a) d -> p b a d", b=2),
                                rden[r, c, :].rearrange("p (b a) -> p b a", b=2).unsqueeze(3)
                                .broadcast_to([BLK, 2, PAIRS, HD]), ALU.mult)
                    last.then_inc(att_done, 1)
                if cur:
                    maxima(0)
                if nxt:
                    dve.wait_ge(xh_done, t + 2)
                    wait(dve, v_done, t + 1)
                    nc.vector.tensor_tensor(xT[1][:, :, :], ps_x, xT[0][:, :, :], ALU.subtract)\
                        .then_inc(xl_done, 1)
                if old:
                    dve.wait_ge(lg_out, t - 1)
                    nc.vector.tensor_reduce(top[:, :], logits[:, :], AX.X, ALU.max).then_inc(top_done, 1)
                if cur:
                    maxima(1)
                if old:
                    dve.wait_ge(top_done, t - 1)
                    nc.vector.scalar_tensor_tensor(pick[:, :], logits[:, :], top[:, :], desc[:, :],
                                                   ALU.is_equal, ALU.mult).then_inc(pick_done, 1)
                if prv:
                    dve.wait_ge(ah_done, t)
                    wait(dve, proj_done, t - 1)
                    nc.vector.tensor_tensor(attT[1][:, :, :, :], ps_aT, attT[0][:, :, :, :], ALU.subtract)\
                        .then_inc(al_done, 1)
                if old:
                    dve.wait_ge(pick_done, t - 1)
                    nc.vector.tensor_reduce(first[:, :], pick[:, :], AX.X, ALU.max).then_inc(first_done, 1)
                if prv:
                    piece, cols = hf + p - 1, slice((1 - p) * I // 2, (2 - p) * I // 2)
                    dve.wait_ge(w1h_done, t)
                    nc.vector.scalar_tensor_tensor(w1s[1][:, piece, cols], w1_in[:, cols], W_UP,
                                                   w1s[0][:, piece, cols], ALU.mult, ALU.subtract)\
                        .then_inc(w1l_done, 1)
                if old:
                    dve.wait_ge(first_done, t - 1)
                    wait(dve, rank_done, t - 2)
                    nc.vector.tensor_scalar(onehot[:, :], desc[:, :], first[:, :], None, ALU.is_equal)\
                        .then_inc(onehot_done, 1)
                if nxt:
                    dve.wait_ge(qkh_done, t + 2)
                    wait(dve, st_done, 4 * t)
                    wait(dve, kcar_done, t)
                    nc.vector.scalar_tensor_tensor(k_[1 - p][:, 1, :, BLK:BLK + P], ps_qk[:, CC:2 * CC, :], W_DOWN,
                                                   k_[1 - p][:, 0, :, BLK:BLK + P], ALU.mult, ALU.subtract)
                    nc.vector.scalar_tensor_tensor(
                        q[:, 1, :, :, :].rearrange("p c b q -> p c (b q)"), ps_qk[:, 0:CC, :], W_DOWN,
                        q[:, 0, :, :, :].rearrange("p c b q -> p c (b q)"), ALU.mult, ALU.subtract)\
                        .then_inc(qkl_done, 1)
                if prv:
                    dve.wait_ge(proj_done, t)
                    dve.wait_ge(xrb_done, t)
                    wait(dve, x1_done, t - 1)
                    nc.vector.scalar_tensor_tensor(y[:, :], ps_m[:, 0:C], W_DOWN, xres[1 - p][:, :],
                                                   ALU.mult, ALU.add).then_inc(y_done, 1)
                if old:
                    dve.wait_ge(rank_done, t - 1)
                    wait(dve, next_done, t - 2)
                    nc.vector.tensor_tensor(place[:, :], ps_rank[:, 0:E], next_slot[:, :], ALU.add)\
                        .then_inc(place_done, 1)
                    nc.vector.tensor_tensor(next_slot[:, :], ps_rank[:, E:2 * E], next_slot[:, :], ALU.add)\
                        .then_inc(next_done, 1)
                if cur:
                    maxima(2)
                if old:
                    dve.wait_ge(place_done, t - 1)
                    dve.wait_ge(onehot_done, t - 1)
                    nc.vector.tensor_tensor(placed[:, :], place[:, :], onehot[:, :], ALU.mult).then_inc(placed_done, 1)
                if prv:
                    dve.wait_ge(y_done, t)
                    nc.vector.bn_stats(stats[:, :], y[:, :]).then_inc(bn_done, 1)
                    apart(dve)
                    dve.wait_ge(bn_done, t)
                    wait(dve, rstd_done, t - 1)
                    nc.vector.bn_aggr(meanvar[:, :], stats[:, :]).then_inc(mv_done, 1)
                if old:
                    dve.wait_ge(placed_done, t - 1)
                    nc.vector.tensor_reduce(slot_f[:, :], placed[:, :], AX.X, ALU.add).then_inc(slotf_done, 1)
                if cur:
                    maxima(3)
                if old:
                    apart(dve)
                    dve.wait_ge(slotf_done, t - 1)
                    wait(dve, disp_st[p], 16 * (hf - 1))
                    nc.vector.tensor_copy(slot_of[p][:, :], slot_f[:, :]).then_inc(slot_done, 1)
                if nxt:
                    dve.wait_ge(qkl_done, t + 2)
                    for n in range(CH):
                        last = nc.vector.tensor_scalar(
                            qbd[1 - p][:, 1, :, :, n, :].rearrange("p c b q -> p (c b) q"),
                            q[:, 1, :, :, :].rearrange("p c b q -> p (c b) q"), band[:, n:n + 1], None, ALU.mult)
                    last.then_inc(qbd_done, 1)
                if prv:
                    dve.wait_ge(rstd_done, t)
                    wait(dve, x1T_done, t - 2)
                    wait(dve, disp_st[1 - p], 16 * (hf + p - 1))
                    nc.vector.tensor_scalar(row[1 - p][:, 0:C], y[:, :], meanvar[:, 0:1], rstd[:, :],
                                            ALU.subtract, ALU.mult).then_inc(x1_done, 1)
                if nxt:
                    dve.wait_ge(v_done, t + 2)
                    if isinstance(t, int) and t < 0:
                        dve.wait_ge(attn_w_ld, 16 * ATTN_LOADS)
                    wait(dve, pv_done, 4 * t)
                    wait(dve, vlow_done, t)
                    wait(dve, vhigh_done, t)
                    nc.vector.scalar_tensor_tensor(
                        v_cur[1 - p][:, :, 0:HD], ps_m[:, 0:C].rearrange("p (h d) -> p h d", h=HEADS), W_DOWN,
                        bv[:, :].rearrange("p (h d) -> p h d", h=HEADS), ALU.mult, ALU.add).then_inc(v_out, 1)
                if isinstance(t, int) and t < 0:
                    later_weights()

            walk_tokens(dve, body)

            step = [0]

            def link(ins):
                step[0] += 1
                ins.then_inc(table_step, 1)
                dve.wait_ge(table_step, step[0])

            dve.wait_ge(next_done, TILES)
            nc.vector.tensor_copy(pad_at[:, :], next_slot[0:1, :]).then_inc(pads_known, 1)
            link(nc.vector.tensor_tensor(total[:, :], next_slot[0:1, :], region_at[:, :], ALU.subtract))
            link(nc.vector.tensor_tensor(over[:, :, :], total[:, :].unsqueeze(2).broadcast_to([1, E, TILES]),
                                         thresholds[:, :, :], ALU.is_gt))
            link(nc.vector.tensor_reduce(ntiles[:, :], over[:, :, :], AX.X, ALU.add))
            nc.vector.tensor_scalar(skip[:, :], ntiles[:, :], -float(P), float(REGION), ALU.mult, ALU.add)
            link(nc.vector.tensor_tensor_scan(tend[:, :], ones_e[:, :], ntiles[:, :], 0.0, ALU.mult, ALU.add))
            link(nc.vector.tensor_tensor(past[:, :, :], tile_no[:, :, :],
                                         tend[:, :].unsqueeze(1).broadcast_to([1, SLOT_TILES, E]), ALU.is_ge))
            link(nc.vector.tensor_tensor(skipped[:, :, :], past[:, :, :],
                                         skip[:, :].unsqueeze(1).broadcast_to([1, SLOT_TILES, E]), ALU.mult))
            link(nc.vector.tensor_reduce(offset[:, :], skipped[:, :, :], AX.X, ALU.add))
            link(nc.vector.scalar_tensor_tensor(base_f[:, :], tile_no[:, :, 0], float(P), offset[:, :],
                                                ALU.mult, ALU.add))
            nc.vector.tensor_copy(base[:, :], base_f[:, :]).then_inc(bases_known, 1)
            link(nc.vector.tensor_reduce(expert_f[:, :], past[:, :, 0:E - 1], AX.X, ALU.add))
            nc.vector.tensor_copy(expert[:, :], expert_f[:, :]).then_inc(slots_known, 1)

            def body3(j, p, hf, load, up, down, norm):
                def split(j, buf, half):
                    a, b = half * IC // 2, (half + 1) * IC // 2
                    dve.wait_ge(hh_done, 2 * j + 1 + half)
                    wait(dve, ffn_done, j - 1)
                    nc.vector.tensor_tensor(h[buf][1][:, a:b, :], g[buf][:, a:b, :], h[buf][0][:, a:b, :],
                                            ALU.subtract).then_inc(hl_done, 1)

                if norm:
                    dve.wait_ge(ffn_done, j)
                    dve.wait_ge(xbo_done, j)
                    wait(dve, ng_done, j - 1)
                    nc.vector.scalar_tensor_tensor(y2, ps_y[1 - p], W_DOWN, xbo[1 - p],
                                                   ALU.mult, ALU.add).then_inc(y2_done, 1)
                    dve.wait_ge(y2_done, j)
                    nc.vector.bn_stats(stats_a[:, :], y2).then_inc(bna_done, 1)
                    apart(dve)
                    dve.wait_ge(bna_done, j)
                    wait(dve, rsa_done, j - 1)
                    nc.vector.bn_aggr(mv_a[:, :], stats_a[:, :]).then_inc(mva_done, 1)
                if down:
                    split(j, p, 1)
                if load:
                    dve.wait_ge(sh_done, j + 3)
                    wait(dve, h_done, 2 * j + 2)
                    nc.vector.tensor_tensor(sT[p][1][:, :, :], ps_sx[p], sT[p][0][:, :, :], ALU.subtract)\
                        .then_inc(sl_done, 1)
                if norm:
                    dve.wait_ge(mva_done, j)
                    wait(dve, z_done, j - 1)
                    nc.vector.scalar_tensor_tensor(ng, y2, mv_a[:, 0:1], gam[:, :],
                                                   ALU.subtract, ALU.mult).then_inc(ng_done, 1)
                    dve.wait_ge(rsa_done, j)
                    dve.wait_ge(ng_done, j)
                    dve.wait_ge(xbe_done, j)
                    wait(dve, fin_done, j - 1)
                    nc.vector.scalar_tensor_tensor(z, ng, rs_a[:, :], xbe[1 - p],
                                                   ALU.mult, ALU.add).then_inc(z_done, 1)
                    dve.wait_ge(z_done, j)
                    nc.vector.bn_stats(stats_b[:, :], z).then_inc(bnb_done, 1)
                    apart(dve)
                    dve.wait_ge(bnb_done, j)
                    wait(dve, rsb_done, j - 1)
                    nc.vector.bn_aggr(mv_b[:, :], stats_b[:, :]).then_inc(mvb_done, 1)
                if up:
                    split(j + 1, 1 - p, 0)
                if norm:
                    apart(dve)
                    dve.wait_ge(token_ld[1 - p], 16 * (hf + p))
                    wait(dve, out_st[1 - p], 16 * (hf + p - 1))
                    nc.vector.tensor_copy(token_i[1 - p][:, :], token[1 - p][:, 1:2]).then_inc(number_out, 1)
                if norm:
                    dve.wait_ge(rsb_done, j)
                    wait(dve, out_st[1 - p], 16 * (hf + p - 1))
                    nc.vector.tensor_scalar(fin[1 - p], z, mv_b[:, 0:1], rs_b[:, :],
                                            ALU.subtract, ALU.mult).then_inc(fin_done, 1)

            walk_slots(dve, body3)

        @block.tensor
        def _(pe):
            mm = nc.tensor.matmul

            def product(dst, left, right, start=True, stop=True):
                terms = [(l, r) for k in range(len(left)) for l, r in
                         ((left[k][0], right[k][0]), (left[k][1], right[k][0]), (left[k][0], right[k][1]))]
                for n, (l, r) in enumerate(terms):
                    last = mm(dst, l, r, start=start and n == 0, stop=stop and n == len(terms) - 1)
                return last

            pe.wait_ge(consts_done, N_CONSTS)

            def setup_transposes():
                pe.wait_ge(ffn_w_ld, 16 * FFN_LOADS)
                for k in range(CC):
                    nc.tensor.transpose(ps[:, 1, k * E:(k + 1) * E], wr_in[:, k * P:(k + 1) * P], ident[0:E, 0:E])
                nc.tensor.transpose(ps[:, 1, P:P + E * IC], b1_in[:, :], ident[0:E * IC, 0:E * IC])\
                    .then_inc(setupT_done, 1)

            def body(t, p, hf, nxt, cur, prv, old):
                var = variant(t) if cur else 0

                def mask(b):
                    return mask_q[:, bass.ds(var, 1), :].rearrange("p a k -> p (a k)") if b == 0 else mask_q[:, 1, :]

                def scores(u):
                    c, b = u // 2, u % 2
                    if u == 0:
                        pe.wait_ge(qbdh_done, t + 1)
                        pe.wait_ge(qbd_done, t + 1)
                        wait(pe, kcar_done, t)
                    wait(pe, mx_done, 4 * t + u - 1)
                    mm(ps_s[u % 2].rearrange("p (a k) -> p a k", a=PAIRS), ident_b[:, :],
                       mask(b).unsqueeze(1).broadcast_to([P, PAIRS, P]),
                       start=True, stop=False, skip_group_check=True)
                    for a in range(PAIRS):
                        last = mm(ps_s[u % 2][:, a * P:(a + 1) * P],
                                  qbd[p][:, 0, c, b, 2 * a:2 * a + 2, :].rearrange("p e q -> p (e q)"),
                                  k_[p][:, 0, c, BLK * b:BLK * b + P],
                                  start=False, stop=a == PAIRS - 1, skip_group_check=True)
                    last.then_inc(s_done, 1)

                def scores_t(u):
                    c, b = u // 2, u % 2
                    wait(pe, exp_done, 4 * t + u - 1)
                    for klo, qlo in ((0, 0), (1, 0), (0, 1)):
                        mm(ps_t[u % 2], k_[p][:, klo, c, BLK * b:BLK * b + P],
                           qbd[p][:, qlo, c, b, :, :].rearrange("p h q -> p (h q)"),
                           start=klo + qlo == 0, stop=False, skip_group_check=True)

                def less_maxima(u):
                    b = u % 2
                    pe.wait_ge(diag_done, 4 * t + u + 1)
                    for e in range(2):
                        left = mask_k[:, e, bass.ds(var, 1), :].rearrange("p a k -> p (a k)") if b == 0 \
                            else mask_k[:, e, 1, :]
                        last = mm(ps_t[u % 2].rearrange("p (a e q) -> p a e q", a=PAIRS, e=2)[:, :, e, :], left,
                                  diag[u % 2][:, e, :, :], start=False, stop=True, skip_group_check=True)
                    last.then_inc(st_done, 1)

                def values(u):
                    c, b = u // 2, u % 2
                    pe.wait_ge(exp_done, 4 * t + u + 1)
                    if u == 0:
                        pe.wait_ge(vhigh_done, t + 1)
                        wait(pe, vlow_done, t)
                        wait(pe, att_done, t)
                    for a in range(PAIRS):
                        h0 = CH * c + 2 * a
                        last = mm(ps_o[:, c, b * PAIRS + a, :], probs[u][:, a, :],
                                  (v_cur if b else v_mid)[p][:, h0:h0 + 2, :].rearrange("p h d -> p (h d)"),
                                  start=True, stop=True)
                    last.then_inc(pv_done, 1)

                if cur:
                    scores(0)
                if old:
                    pe.wait_ge(x1T_out, t - 1)
                    if cur:
                        pe.wait_ge(v_out, t + 1)
                    for k in range(CC):
                        last = mm(ps_m[:, 0:E], x1T[:, k, :], wrT[:, k, :], start=k == 0, stop=k == CC - 1)
                    last.then_inc(lg_done, 1)
                if nxt:
                    pe.wait_ge(xin_ld[1 - p], 16 * (hf + p + 1))
                    wait(pe, x1T_out, t - 1)
                    for k in range(CC):
                        last = nc.tensor.transpose(ps_x[:, k, :], xin[1 - p][:, k * P:(k + 1) * P], ident[:, :])
                    last.then_inc(xT_done, 1)
                if cur:
                    scores_t(0)
                    scores(1)
                if prv:
                    pe.wait_ge(att_done, t)
                    wait(pe, lg_out, t - 1)
                    for b in range(2):
                        last = nc.tensor.transpose(ps_m[:, b * P:(b + 1) * P],
                                                   att[:, b, :, :, :].rearrange("p c a d -> p (c a d)"),
                                                   ident[:, :])
                    last.then_inc(attT_done, 1)
                if nxt:
                    pe.wait_ge(xl_done, t + 2)
                    if isinstance(t, int) and t < 0:
                        pe.wait_ge(wlo_done, 2)
                    for m in range(2 * CC):
                        cols = slice(m * P, (m + 1) * P)
                        mm(ps_qk[:, m, :], bqk[:, cols], ones16[:, :], start=True, stop=False)
                        last = product(ps_qk[:, m, :], [(wa[0][:, k, cols], wa[1][:, k, cols]) for k in range(CC)],
                                       [(xT[0][:, k, :], xT[1][:, k, :]) for k in range(CC)], start=False)
                    last.then_inc(qk_done, 1)
                if isinstance(t, int) and t < 0:
                    setup_transposes()
                if cur:
                    less_maxima(0)
                if old:
                    pe.wait_ge(onehot_done, t - 1)
                    if prv:
                        pe.wait_ge(al_done, t)
                    else:
                        pe.wait_ge(lg_out, t - 1)
                    mm(ps_rank[:, 0:E], before[:, :], onehot[:, :], start=True, stop=True)
                    mm(ps_rank[:, E:2 * E], ones_b[:, :], onehot[:, :], start=True, stop=True).then_inc(rank_done, 1)
                if prv:
                    pe.wait_ge(al_done, t)
                    if isinstance(t, int):
                        pe.wait_ge(wlo_done, 4)
                    product(ps_m[:, 0:C], [tuple(attT[s][:, e, :, :].rearrange("p b q -> p (b q)") for s in range(2))
                                            for e in range(2)],
                            [(wp[0][:, e, :], wp[1][:, e, :]) for e in range(2)]).then_inc(proj_done, 1)
                if cur:
                    scores(2)
                    scores_t(1)
                    less_maxima(1)
                    scores(3)
                    values(0)
                    scores_t(2)
                    less_maxima(2)
                    values(1)
                    scores_t(3)
                    less_maxima(3)
                if nxt:
                    wait(pe, y_done, t)
                    wait(pe, next_done, t - 1)
                    if isinstance(t, int) and t < 0:
                        pe.wait_ge(setupT_out, 1)
                    product(ps_m[:, 0:C], [(xT[0][:, k, :], xT[1][:, k, :]) for k in range(CC)],
                            [(wa[0][:, k, 2 * C:3 * C], wa[1][:, k, 2 * C:3 * C]) for k in range(CC)])\
                        .then_inc(v_done, 1)
                if cur:
                    values(2)
                if prv:
                    pe.wait_ge(x1_done, t)
                    wait(pe, qkl_done, t + 2 if nxt else 0)
                    for k in range(CC):
                        last = nc.tensor.transpose(ps_x[:, k, :], row[1 - p][:, k * P:(k + 1) * P], ident[:, :])
                    last.then_inc(x1T_done, 1)
                if cur:
                    values(3)

            walk_tokens(pe, body)

            TURNS = 17

            def body3(j, p, hf, load, up, down, norm):
                if load:
                    pe.wait_ge(xa_ld[p], 16 * (hf + 2))
                    wait(pe, sl_done, j + 1)
                    for k in range(CC):
                        last = nc.tensor.transpose(ps_sx[p][:, k, :], xa[p][:, k * P:(k + 1) * P], ident[:, :])
                    last.then_inc(sT_done, 1)
                if up:
                    e = pe.value_load(expert[0:1, bass.ds(j + 1, 1)], min_val=0, max_val=E - 1)
                    pe.wait_ge(sl_done, j + 2)

                def weights(s, k, ic):
                    return w1s[s][:, bass.ds(e * CC + k, 1), ic * P:(ic + 1) * P].rearrange("p a i -> p (a i)")

                if down:
                    wait(pe, y2_done, j - 1)

                def output(first, last):
                    for n in range(first, last):
                        ic, (hs, ws) = n // 3, ((0, 0), (1, 0), (0, 1))[n % 3]
                        if n in (0, 3 * IC // 2):
                            pe.wait_ge(hl_done, 2 * j + 1 + (n > 0))
                        ins = mm(ps_y[p], h[p][hs][:, ic, :], wo[ws][:, ic, :], start=n == 0, stop=n == 3 * IC - 1)
                        if n == 3 * IC - 1:
                            ins.then_inc(ffn_done, 1)

                for ic in range(IC):
                    half, col = ic // (IC // 2), (ic % (IC // 2)) * P
                    if up and col == 0:
                        wait(pe, g_done, 2 * j - 1 + half)
                    for k in range(CC):
                        if up:
                            for n, (ws, ss) in enumerate(((0, 0), (1, 0), (0, 1))):
                                up_ins = mm(ps_h[1 - p][:, half, col:col + P], weights(ws, k, ic),
                                            sT[1 - p][ss][:, k, :], start=k + n == 0, stop=k == CC - 1 and n == 2)
                            if col == (IC // 2 - 1) * P and k == CC - 1:
                                up_ins.then_inc(h_done, 1)
                        if down:
                            g0 = ic * CC + k
                            output(g0 * TURNS // (IC * CC), (g0 + 1) * TURNS // (IC * CC))
                if down:
                    output(TURNS, 3 * IC)

            pe.wait_ge(slots_known, 1)
            pe.wait_ge(w1l_done, TILES)
            walk_slots(pe, body3)


_INS = ['L0_attn_x', 'L0_attn_W_attn', 'L0_attn_b_attn', 'L0_attn_W_proj', 'L0_attn_b_proj', 'L0_ffn_Wr',
        'L0_ffn_W1', 'L0_ffn_b1', 'L0_ffn_Wo', 'L0_ffn_bo', 'L0_ffn_gamma', 'L0_ffn_beta']
_OUTS = [((2, 2048, 256), 'float32')]


def kernel(**inputs):
    import numpy as _np
    import concourse.bacc as _bacc
    from concourse import mybir as _mybir
    from concourse.bass_utils import run_bass_kernel_spmd as _run

    nc = _bacc.Bacc("TRN2", target_bir_lowering=False, num_devices=1)
    arrays, args = {}, []
    for name in _INS:
        a = _np.ascontiguousarray(inputs[name])
        arrays[f"in_{name}_dram"] = a
        args.append(nc.dram_tensor(f"in_{name}_dram", a.shape, _mybir.dt.from_np(a.dtype), kind="ExternalInput").ap())
    for i, (shape, dtype) in enumerate(_OUTS):
        dt = _mybir.dt.from_np(_np.dtype(dtype))
        args.append(nc.dram_tensor(f"out_{i}_dram", shape, dt, kind="ExternalOutput").ap())
    attention_then_routed_ffn(nc, *args)
    r = _run(nc, [arrays], core_ids=[0])
    got = tuple(r.results[0][f"out_{i}_dram"] for i in range(len(_OUTS)))
    return got[0]
```
